# Optimizing a Trainium2 kernel written in Bass

```python
import numpy as np
import jax
import jax.numpy as jnp

def _softmax(x, axis=-1):
    return jax.nn.softmax(x, axis=axis)

def _gelu(x):
    return jax.nn.gelu(x, approximate=True)

def _silu(x):
    return jax.nn.silu(x)

def _sigmoid(x):
    return jax.nn.sigmoid(x)

def _layernorm(x, axis=-1, eps=1e-05):
    m = jnp.mean(x, axis=axis, keepdims=True)
    v = jnp.var(x, axis=axis, keepdims=True)
    return (x - m) / jnp.sqrt(v + eps)

def _scatter_add(tgt, idx, src, axis=0):
    return tgt.at[idx].add(src)

def _segment_sum(src, seg, n):
    return jax.ops.segment_sum(src, seg, n)
kernel_name = 'mk_recurrent_d1_jaxref_r4_74a9dc'

def setup_inputs(seed: int=0):
    np.random.seed(seed)
    _w = jnp.asarray

    def _L0_attn_setup():
        import jax, jax.numpy as jnp
        import numpy as np
        D_MODEL = 256
        N_HEADS = 16
        D_LATENT = 64
        HEAD_DIM = D_MODEL // N_HEADS

        def apply_rope(x):
            B, T, H, D = x.shape
            inv_freq = 1.0 / 10000.0 ** (jnp.arange(0, D, 2, dtype=jnp.float32) / D)
            t = jnp.arange(T, dtype=jnp.float32)
            freqs = t[:, None] * inv_freq[None, :]
            sin_f = jnp.sin(freqs)[None, :, None, :]
            cos_f = jnp.cos(freqs)[None, :, None, :]
            x1, x2 = jnp.split(x, 2, axis=-1)
            return jnp.concatenate([x1 * cos_f - x2 * sin_f, x1 * sin_f + x2 * cos_f], axis=-1)
        key = jax.random.key(seed)
        ks = jax.random.split(key, 10)
        B, T = (4, 1024)
        s = lambda fan_in: 1.0 / np.sqrt(fan_in)
        return {'x': jax.random.normal(ks[0], (B, T, D_MODEL), dtype=jnp.float32), 'Wq': jax.random.normal(ks[1], (D_MODEL, D_MODEL), dtype=jnp.float32) * s(D_MODEL), 'bq': jnp.zeros((D_MODEL,), jnp.float32), 'Wdown': jax.random.normal(ks[2], (D_MODEL, D_LATENT), dtype=jnp.float32) * s(D_MODEL), 'bdown': jnp.zeros((D_LATENT,), jnp.float32), 'Wup': jax.random.normal(ks[3], (D_LATENT, 2 * D_MODEL), dtype=jnp.float32) * s(D_LATENT), 'bup': jnp.zeros((2 * D_MODEL,), jnp.float32), 'Wout': jax.random.normal(ks[4], (D_MODEL, D_MODEL), dtype=jnp.float32) * s(D_MODEL), 'bout': jnp.zeros((D_MODEL,), jnp.float32)}
    _L0_attn_in = _L0_attn_setup()

    def _L0_ffn_setup():
        import jax, jax.numpy as jnp
        import numpy as np
        NUM_HEADS = 16
        TOP_K = 2
        key = jax.random.key(seed)
        ks = jax.random.split(key, 5)
        B, S, D, E = (4, 512, 256, 8)
        scale = 0.02
        return {'x': jax.random.normal(ks[0], (B, S, D), dtype=jnp.float32), 'W_qkv': jax.random.normal(ks[1], (D, 3 * D), dtype=jnp.float32) * scale, 'b_qkv': jnp.zeros((3 * D,), dtype=jnp.float32), 'W_gate': jax.random.normal(ks[2], (D, E), dtype=jnp.float32) * scale, 'b_gate': jnp.zeros((E,), dtype=jnp.float32), 'W_experts': jax.random.normal(ks[3], (E, D, D), dtype=jnp.float32) * scale, 'b_experts': jnp.zeros((E, D), dtype=jnp.float32)}
    _L0_ffn_in = _L0_ffn_setup()
    _d = {'L0_attn_x': _L0_attn_in['x'], 'L0_attn_Wq': _L0_attn_in['Wq'], 'L0_attn_bq': _L0_attn_in['bq'], 'L0_attn_Wdown': _L0_attn_in['Wdown'], 'L0_attn_bdown': _L0_attn_in['bdown'], 'L0_attn_Wup': _L0_attn_in['Wup'], 'L0_attn_bup': _L0_attn_in['bup'], 'L0_attn_Wout': _L0_attn_in['Wout'], 'L0_attn_bout': _L0_attn_in['bout'], 'L0_ffn_W_qkv': _L0_ffn_in['W_qkv'], 'L0_ffn_b_qkv': _L0_ffn_in['b_qkv'], 'L0_ffn_W_gate': _L0_ffn_in['W_gate'], 'L0_ffn_b_gate': _L0_ffn_in['b_gate'], 'L0_ffn_W_experts': _L0_ffn_in['W_experts'], 'L0_ffn_b_experts': _L0_ffn_in['b_experts']}
    _x0 = _d['L0_attn_x']
    _d['L0_attn_x'] = jax.random.normal(jax.random.fold_in(jax.random.key(seed), 1), (8, 512, 256), dtype=_x0.dtype)
    del _x0
    return _d

def reference(L0_attn_x, L0_attn_Wq, L0_attn_bq, L0_attn_Wdown, L0_attn_bdown, L0_attn_Wup, L0_attn_bup, L0_attn_Wout, L0_attn_bout, L0_ffn_W_qkv, L0_ffn_b_qkv, L0_ffn_W_gate, L0_ffn_b_gate, L0_ffn_W_experts, L0_ffn_b_experts):

    def _L0_attn_ref(x, Wq, bq, Wdown, bdown, Wup, bup, Wout, bout):
        import jax, jax.numpy as jnp
        import numpy as np
        D_MODEL = 256
        N_HEADS = 16
        D_LATENT = 64
        HEAD_DIM = D_MODEL // N_HEADS

        def apply_rope(x):
            B, T, H, D = x.shape
            inv_freq = 1.0 / 10000.0 ** (jnp.arange(0, D, 2, dtype=jnp.float32) / D)
            t = jnp.arange(T, dtype=jnp.float32)
            freqs = t[:, None] * inv_freq[None, :]
            sin_f = jnp.sin(freqs)[None, :, None, :]
            cos_f = jnp.cos(freqs)[None, :, None, :]
            x1, x2 = jnp.split(x, 2, axis=-1)
            return jnp.concatenate([x1 * cos_f - x2 * sin_f, x1 * sin_f + x2 * cos_f], axis=-1)
        B, T, D = x.shape
        H, Dh = (N_HEADS, HEAD_DIM)
        q = x @ Wq + bq
        kv_latent = x @ Wdown + bdown
        kv = kv_latent @ Wup + bup
        q = q.reshape(B, T, H, Dh)
        kv = kv.reshape(B, T, H, 2 * Dh)
        k, v = jnp.split(kv, 2, axis=-1)
        q = apply_rope(q)
        k = apply_rope(k)
        att = jnp.einsum('bthd,btgd->bthg', q, k) / jnp.sqrt(jnp.float32(Dh))
        att = jax.nn.softmax(att, axis=-1)
        out = jnp.einsum('bthg,btgd->bthd', att, v)
        out = out.reshape(B, T, D)
        return out @ Wout + bout

    def _L0_ffn_ref(x, W_qkv, b_qkv, W_gate, b_gate, W_experts, b_experts):
        import jax, jax.numpy as jnp
        import numpy as np
        NUM_HEADS = 16
        TOP_K = 2
        B, S, D = x.shape
        H = NUM_HEADS
        hd = D // H
        E = W_gate.shape[-1]
        qkv = (x @ W_qkv + b_qkv).reshape(B, S, 3, H, hd)
        q, k, v = (qkv[:, :, 0], qkv[:, :, 1], qkv[:, :, 2])
        attn = jnp.einsum('bqhd,bkhd->bhqk', q, k) / jnp.sqrt(jnp.asarray(hd, x.dtype))
        attn = jax.nn.softmax(attn, axis=-1)
        attn_out = jnp.einsum('bhqk,bkhd->bqhd', attn, v).reshape(B, S, D)
        gate = jax.nn.softmax(x @ W_gate + b_gate, axis=-1)
        top_g, top_i = jax.lax.top_k(gate, TOP_K)
        combine = jnp.sum(jax.nn.one_hot(top_i, E, dtype=x.dtype) * top_g[..., None], axis=2)
        expert_out = jnp.einsum('bsd,edf->bsef', x, W_experts) + b_experts
        moe_out = jnp.einsum('bsef,bse->bsf', expert_out, combine)
        return attn_out + moe_out
    x = L0_attn_x
    xn = _layernorm(x, axis=-1)
    s = _L0_attn_ref(xn, L0_attn_Wq, L0_attn_bq, L0_attn_Wdown, L0_attn_bdown, L0_attn_Wup, L0_attn_bup, L0_attn_Wout, L0_attn_bout)
    g = _silu(_L0_ffn_ref(xn, L0_ffn_W_qkv, L0_ffn_b_qkv, L0_ffn_W_gate, L0_ffn_b_gate, L0_ffn_W_experts, L0_ffn_b_experts))
    x = x + s * g
    return x

_drawn_inputs = setup_inputs


def setup_inputs(seed=0):
    import zlib

    import numpy as np

    out = dict(_drawn_inputs(seed))
    spreads = {'L0_attn_bq': (0.0, 0.8),
     'L0_attn_bdown': (0.0, 0.8),
     'L0_attn_bup': (0.0, 0.8),
     'L0_attn_bout': (0.0, 0.8),
     'L0_ffn_b_qkv': (0.0, 0.419),
     'L0_ffn_b_gate': (0.0, 0.8),
     'L0_ffn_b_experts': (0.0, 0.8)}
    factors = {'L0_attn_Wq': 3.16, 'L0_ffn_W_qkv': 8.0, 'L0_ffn_W_gate': 3.948, 'L0_ffn_W_experts': 3.573}
    for name, (base, spread) in spreads.items():
        noise = np.random.default_rng([zlib.crc32(name.encode()), seed]).standard_normal(out[name].shape)
        drawn = base * np.exp(spread * noise) if base else spread * noise
        out[name] = jnp.asarray(drawn.astype(out[name].dtype))
    for name, factor in factors.items():
        out[name] = (out[name] * factor).astype(out[name].dtype)
    return out
```

```python
from contextlib import ExitStack

import concourse.bass as bass
from concourse import mybir

ALU = mybir.AluOpType
ACT = mybir.ActivationFunctionType
AX = mybir.AxisListType.X
F32 = mybir.dt.float32
F32R = mybir.dt.float32r
BF16 = mybir.dt.bfloat16
U32 = mybir.dt.uint32

P = 128
EPS = 1e-5
SLOTS = 16
GROUP = 4
PRODUCTS = 6
Q_PARTS = (0, 0, 1, 1, 0, 2)
K_PARTS = (0, 1, 0, 1, 2, 0)
STACK_DMAS = 2 * PRODUCTS
QK_SLOT = {6: 0, 7: 1, 13: 2, 14: 3}


def wait(engine, semaphore, count):
    if not isinstance(count, int) or count > 0:
        engine.wait_ge(semaphore, count)


def wait_apart(engine, passed, semaphore, count):
    wait(engine, semaphore, count)
    if not isinstance(count, int):
        engine.sem_inc(passed, 1)


def front_bank_users(s, prev, body, nxt):
    early = late = None
    if s % 4 == 0 and body:
        early = "bias"
    if s % 4 == 1 and (prev if s == 1 else body):
        early = "attn"
    if s % 4 == 2 and (nxt if s == 14 else body):
        early = "max"
    if nxt:
        if s == 15:
            early = "latent"
        late = {2: "xT", 3: "xT", 4: "xT", 5: "xT", 6: "qk", 7: "qk", 9: "v", 10: "v", 11: "v", 12: "v",
                13: "qk", 14: "qk", 15: "gateT"}.get(s)
    return early, late


def build(nc, x, Wq, bq, Wdown, bdown, Wup, bup, Wout, bout, W_qkv, b_qkv, W_gate, b_gate, W_experts, b_experts, out):
    B, T, D = x.shape
    E = W_gate.shape[1]
    L = Wdown.shape[1]
    H = 16
    DH = D // H
    TILES = T // P
    CH = D // P
    HC = H // CH
    assert (TILES, CH, H, E, 2 * L, GROUP) == (4, 2, 16, 8, P, 4) and B % 2 == 0
    ROWS = PRODUCTS * DH + 3
    SCALE = float(DH) ** -0.5
    HALF = H * H * DH // 2
    STACKED = 16 * STACK_DMAS

    QK, VG, DD, MQ, EX, WO = 0, 512, 776, 904, 1160, 3208
    NW = WO + D
    pieces = [(QK, 512), (VG, D + E), (DD, 2 * L), (MQ, D)] + [(EX + 512 * e, 512) for e in range(E // 2)] + [(WO, D)]
    PIECE = {start: n + 1 for n, (start, _) in enumerate(pieces)}

    with ExitStack() as ctx:
        def sb(name, shape, dt=F32):
            return ctx.enter_context(nc.sbuf_tensor(name, shape, dt))

        def bank(name, shape):
            return ctx.enter_context(nc.psum_tensor(name, shape, F32))

        def sem(name):
            return ctx.enter_context(nc.semaphore(name))

        w_hi = sb("w_hi", [P, CH, NW], F32R)
        w_lo = sb("w_lo", [P, CH, NW], F32R)
        up_hi = sb("up_hi", [P, 2 * D], F32R)
        up_lo = sb("up_lo", [P, 2 * D], F32R)
        eb = sb("eb", [4 * E, D], F32R)
        scratch = sb("scratch", [P, 8192])
        stage = scratch[:, 0:CH * NW].rearrange("p (c n) -> p c n", c=CH)
        up_stage = scratch[:, CH * NW:CH * NW + 2 * D]
        eb_stage = scratch[0:4 * E, CH * NW + 2 * D:CH * NW + 3 * D]
        eb_low = scratch[0:4 * E, CH * NW + 3 * D:CH * NW + 4 * D].bitcast(F32R)
        probs = scratch[:, 0:4096].rearrange("p (s i q) -> p s i q", s=2, i=GROUP)
        prod = scratch[:, 4096:8192].rearrange("p (s n) -> p s n", s=2)
        assert CH * NW + 4 * D <= 8192
        ident = sb("ident", [P, P])
        iota = sb("iota", [P, TILES, E])
        half = sb("half", [P, TILES])
        bqk = sb("bqk", [P, 4])
        bdd = sb("bdd", [P, 1])
        bq_all = sb("bq_all", [P, D])
        bup_all = sb("bup_all", [P, 2 * D])
        bvg_all = sb("bvg_all", [P, D + E])
        bout_all = sb("bout_all", [P, D])

        x_in = sb("x_in", [P, TILES, D])
        x_fin = sb("x_fin", [P, 2, D])
        stats = sb("stats", [P, TILES, 6])
        meanvar = sb("meanvar", [P, TILES, 2])
        vareps = sb("vareps", [P, TILES])
        rstd = sb("rstd", [P, TILES])
        xT_hi = sb("xT_hi", [P, 2, CH, T], F32R)
        xT_lo = sb("xT_lo", [P, 2, CH, T], F32R)
        parts = sb("parts", [P, 2, 3, T], BF16)
        rest = sb("rest", [P, T])
        q_stack = sb("q_stack", [ROWS, H, T], BF16)
        k_stack = sb("k_stack", [ROWS, H, T], BF16)
        v_one = sb("v_one", [P, 2, TILES, H, DH + 1])
        logits = sb("logits", [P, TILES, E])
        gsum = sb("gsum", [P, TILES])
        gshift = sb("gshift", [P, TILES, E])
        gate = sb("gate", [P, TILES, E])
        top = sb("top", [P, TILES, 8])
        topi = sb("topi", [P, TILES, 8], U32)
        topf = sb("topf", [P, TILES, 2])
        pick = sb("pick", [P, 2, TILES, E])
        combine = sb("combine", [P, 2, TILES, E])
        c_hi = sb("c_hi", [P, TILES, E], F32R)
        c_parts = sb("c_parts", [P, TILES, 4, E])
        cT = sb("cT", [4 * E, T], F32R)
        latent = sb("latent", [P, T], F32R)

        negmax = sb("negmax", [P, 2, 16])
        mrest = sb("mrest", [16, P])
        mparts = sb("mparts", [16, 2, 3, P], BF16)
        av = sb("av", [P, T])
        arec = sb("arec", [P, TILES, GROUP])
        attn = sb("attn", [P, TILES, D])
        scaled = sb("scaled", [P, 2, D])
        z = sb("z", [P, 2, TILES, D])

        mq = sb("mq", [P, D])
        mkv = sb("mkv", [P, 2, 2, D])
        msc = sb("msc", [P, 2, H, H])
        mmax = sb("mmax", [P, H])
        msum = sb("msum", [P, H])
        mrec = sb("mrec", [P, 2, H])
        mo = sb("mo", [P, D])
        moT_hi = sb("moT_hi", [P, CH, P], F32R)
        moT_lo = sb("moT_lo", [P, CH, P], F32R)
        s_mla = sb("s_mla", [P, TILES, D])
        th = sb("th", [P, 2, D])

        p1 = [bank(f"p1_{i}", [P, T]) for i in range(2)]
        p2 = [bank(f"p2_{i}", [P, T]) for i in range(2)]
        p_av = bank("p_av", [P, T])
        p_moe = bank("p_moe", [P, 2, D])
        p_mla = bank("p_mla", [P, 2 * D])
        p_front = bank("p_front", [P, T])

        names = """st_done max_scores_done av_done moe_done mq_done mkv_done moT_done wo_done xT_done qk_done v_done latent_done
            gateT_done bias_done maxT_done attnT_done
            exp_done part1_done part2_done xhi_done lat_hi_done gexp_done cT_done z_begun mexp_done mohi_done m1_done
            av_out tanh_done scaled_done whi_done
            max_done stats_done meanvar_done xn_done xlo_done rest_done v_out logits_out gmax_done gshift_done gsum_done grec_done
            gate_done top_done topi_done topf_done pick_done picks_done combine_done chi_done clo_done cparts_done
            lat_lo_done mrest_done m2_done m3_done arec_done attn_out mq_out mkv_out scores_reduced values_reduced mmax_done mshift_done msum_done
            mrec_done mo_out molo_done s_out g_done w_done wlo_done eblo_done av_zeroed
            score_products value_products moe_one moe_added ve_done rstd_done part3_done z_ready res_done consts_done ident_zeroed iota_done half_done ones_done
            x_loaded bup_done dve_passed pool_passed sp_passed vones_done eb_ready bias_loaded""".split()
        S = {n: sem(n) for n in names}
        w_loaded = [sem(f"w_loaded{n}") for n in range(len(pieces) + 2)]
        stacked = [sem("stacked0"), sem("stacked1")]
        mrows = [sem("mrows0"), sem("mrows1")]
        xfin_loaded = [sem("xfin_loaded0"), sem("xfin_loaded1")]
        stored = [sem("stored0"), sem("stored1")]

        x_v = x.rearrange("b (t p) d -> b p t d", p=P)
        out_v = out.rearrange("b (t p) d -> b p t d", p=P)

        block = ctx.enter_context(nc.Block())

        def weight_views(w, start, width):
            if start != QK:
                return [(w[:, :, start:start + width], stage[:, :, start:start + width])]
            return [(w[:, c, QK:QK + width].rearrange("p (k d h) -> p k d h", d=DH, h=HC),
                     stage[:, c, QK:QK + width].rearrange("p (k h d) -> p k d h", d=DH, h=HC)) for c in range(CH)]

        def up_views(to, src):
            src = src.rearrange("p (h r d) -> p r h d", r=2, d=DH)
            return [(to[:, 0:D].rearrange("p (h d) -> p h d", h=H), src[:, 0]),
                    (to[:, D:2 * D].rearrange("p (d h) -> p h d", h=H), src[:, 1])]

        def batches(engine, slot):
            for s in range(SLOTS):
                slot(-1, s, 1, False, False, True)
            for s in range(SLOTS):
                slot(0, s, 0, False, True, True)
            with engine.Fori(0, (B - 2) // 2) as i:
                for par in (1, 0):
                    for s in range(SLOTS):
                        slot(2 * i + (1 if par else 2), s, par, True, True, True)
            for s in range(SLOTS):
                slot(B - 1, s, 1, True, True, False)
            for s in range(8):
                slot(B, s, 0, True, False, False)

        def max_unit(b, s, body, nxt):
            there = body if s <= 9 else nxt
            return there, 16 * b + s + 6, ((s + 6) // 4) % 4, (s + 2) % 4

        @block.sync
        def _(sp):
            def sp_wait(semaphore, count):
                wait_apart(sp, S["sp_passed"], semaphore, count)

            def load_weights():
                sp.dma_start(x_in[:], x_v[0]).then_inc(S["x_loaded"], 16)
                for n, (start, width) in enumerate(pieces):
                    to = stage[:, :, start:start + width]
                    if start == QK:
                        srcs = [(to, W_qkv[:, 0:512])]
                    elif start == VG:
                        srcs = [(to[:, :, 0:D], W_qkv[:, 2 * D:3 * D]), (to[:, :, D:D + E], W_gate)]
                    elif start == DD:
                        srcs = [(to[:, :, 0:L], Wdown), (to[:, :, L:2 * L], Wdown)]
                    elif start == MQ:
                        srcs = [(to, Wq)]
                    elif start == WO:
                        srcs = [(to, Wout)]
                    else:
                        e = (start - EX) // D
                        srcs = [(to[:, :, 0:D], W_experts[e]), (to[:, :, D:2 * D], W_experts[e + 1])]
                    for dst, src in srcs:
                        sp.dma_start(dst, src.rearrange("(c p) n -> p c n", p=P)).then_inc(w_loaded[n], 16)
                    if start == QK:
                        for i in range(4):
                            src = b_qkv[(i % 2) * D + (i // 2) * P:][0:P].rearrange("(h d) -> d h", h=HC)
                            sp.dma_start(bqk[:, i:i + 1], src, allow_slow_non_contiguous=True).then_inc(S["bias_loaded"], 16)
                        for r in range(2):
                            sp.dma_start(bdd[L * r:L * r + L, :], bdown.rearrange("(a n) -> n a", a=1), allow_slow_non_contiguous=True).then_inc(S["bias_loaded"], 16)
                        for dst, src in ((bvg_all[:, 0:D], b_qkv[2 * D:3 * D]), (bvg_all[:, D:D + E], b_gate), (bq_all[:], bq),
                                         (rest[:], bup), (bout_all[:], bout)):
                            n_src = src.shape[0]
                            sp.dma_start(dst, src.rearrange("(a n) -> a n", a=1).broadcast_to([P, n_src])).then_inc(S["bias_loaded"], 16)
                for r in range(2):
                    sp.dma_start(up_stage[L * r:L * r + L, :], Wup).then_inc(w_loaded[-2], 16)
                for r in range(4):
                    sp.dma_start(eb_stage[E * r:E * r + E, :], b_experts).then_inc(w_loaded[-1], 16)

            def stack(c, b):
                sp_wait(S["part3_done"], 4 * b + 2 * c + 2)
                sp_wait(S["st_done"], 64 * b - (32 if c == 0 else 0))
                heads = slice(HC * c, HC * c + HC)
                for r in range(PRODUCTS):
                    for to, which, part in ((q_stack, 0, Q_PARTS[r]), (k_stack, 1, K_PARTS[r])):
                        sp.dma_start(to[DH * r:DH * r + DH, heads, :], parts[:, which, part, :]).then_inc(stacked[c], 16)

            def slot(b, s, par, prev, body, nxt):
                if s == 0 and body and nxt:
                    sp_wait(S["xT_done"], 4 * (b + 1))
                    sp.dma_start(x_in[:], x_v[b + 1]).then_inc(S["x_loaded"], 16)
                if s == 0 and body:
                    stack(1, b)
                if s == 8 and nxt:
                    stack(0, b + 1)
                if prev and 3 <= s <= 6:
                    t = s - 3
                    sp_wait(stored[t % 2], 16 * (2 * (b - 1) + t // 2))
                    sp.dma_start(x_fin[:, t % 2, :], x_v[b - 1][:, t, :]).then_inc(xfin_loaded[t % 2], 16)
                if s % 4 == 2 and (nxt if s == 14 else body):
                    g = (s // 4 + 1) % 4
                    n = 4 * b + s // 4 + 1
                    sp_wait(S["m3_done"], n + 1)
                    for r in range(3):
                        row = PRODUCTS * DH + r
                        sp.dma_start(q_stack[row:row + 1, GROUP * g:GROUP * g + GROUP, :], mparts[:, g % 2, r, :]).then_inc(mrows[g % 2], 16)
                if prev and 4 <= s <= 7:
                    t = s - 4
                    sp_wait(S["res_done"], 4 * (b - 1) + t + 1)
                    sp.dma_start(out_v[b - 1][:, t, :], x_fin[:, t % 2, :]).then_inc(stored[t % 2], 16)

            load_weights()
            sp.wait_ge(S["eblo_done"], 1)
            sp.dma_start(eb[2 * E:4 * E, :].bitcast(F32), eb_low[2 * E:4 * E, :].bitcast(F32)).then_inc(S["eb_ready"], 16)
            batches(sp, slot)
            for p in range(2):
                sp.wait_ge(stored[p], 16 * 2 * B)

        @block.tensor
        def _(pe):
            def front_bank_free(b, s, late, prev, body, nxt):
                at, name = s, front_bank_users(s, prev, body, nxt)[0] if late else None
                while at > 0 and not name:
                    at -= 1
                    name = next((user for user in reversed(front_bank_users(at, prev, body, nxt)) if user), None)
                if not name:
                    if isinstance(b, int) and b == -1:
                        return
                    if isinstance(b, int) and b == B:
                        pe.wait_ge(S["attn_out"], TILES * B - 1)
                    else:
                        pe.wait_ge(S["cT_done"], b + 1)
                    return
                t = at // 4
                semaphore, count = {
                    "attn": ("attn_out", 4 * b + t),
                    "bias": ("z_begun", 4 * b + t + 1),
                    "max": ("mrest_done", 4 * b + t + 2),
                    "xT": ("xlo_done", 4 * (b + 1) + at - 1),
                    "qk": ("rest_done", 4 * (b + 1) + QK_SLOT.get(at, 0) + 1),
                    "v": ("logits_out", 4 * (b + 1) + at - 8),
                    "latent": ("lat_lo_done", b + 2),
                    "gateT": ("cT_done", b + 2),
                }[name]
                wait(pe, S[semaphore], count)

            def split_matmul(to, xs, ws, done=None):
                n = 0
                for c in range(CH):
                    for i, j in ((0, 0), (0, 1), (1, 0)):
                        last = pe.matmul(to, xs(c)[i], ws(c)[j], start=(n == 0), stop=(n == 3 * CH - 1))
                        n += 1
                last.then_inc(S[done], 1)

            def weights(start, width):
                return lambda c: (w_hi[:, c, start:start + width], w_lo[:, c, start:start + width])

            def x_tile(par, t):
                return lambda c: (xT_hi[:, par, c, P * t:P * t + P], xT_lo[:, par, c, P * t:P * t + P])

            def x_row(par):
                return lambda c: (xT_hi[:, par, c, :], xT_lo[:, par, c, :])

            def scores_t(b, g, kt, s, i):
                n = 64 * b + 4 * s + i
                wait(pe, S["exp_done"], n - 1)
                h = GROUP * g + i
                pe.matmul(p2[i % 2][:, :], k_stack[:, h, P * kt:P * kt + P], q_stack[:, h, :],
                          start=True, stop=True).then_inc(S["st_done"], 1)

            def max_scores(u, g, i, qt):
                wait(pe, S["max_done"], 4 * u + qt - 1)
                h = GROUP * g + i
                pe.matmul(p1[qt % 2][:, :], q_stack[0:PRODUCTS * DH, h, P * qt:P * qt + P], k_stack[0:PRODUCTS * DH, h, :],
                          start=True, stop=True).then_inc(S["max_scores_done"], 1)

            def front(b, s, par, name):
                b1, par1 = b + 1, 1 - par
                if name == "attn":
                    wait(pe, S["av_out"], 4 * b + s // 4)
                    for qt in range(TILES):
                        last = pe.transpose(p_front[:, P * qt:P * qt + P], av[:, P * qt:P * qt + P], ident[:])
                    last.then_inc(S["attnT_done"], 1)
                if name == "bias":
                    if s == 0:
                        wait(pe, S["cT_done"], b + 1)
                    t = s // 4
                    pe.matmul(p_front[:, 0:D], cT[:, P * t:P * t + P], eb[:], start=True, stop=True).then_inc(S["bias_done"], 1)
                if name == "max":
                    g = (s // 4 + 1) % 4
                    wait(pe, S["max_done"], 16 * (4 * b + s // 4 + 2))
                    pe.transpose(p_front[0:16, 0:P], negmax[:, g % 2, :], ident[:]).then_inc(S["maxT_done"], 1)
                if name == "xT":
                    t = s - 2
                    wait(pe, S["xn_done"], 4 * b1 + t + 1)
                    for c in range(CH):
                        last = pe.transpose(p_front[:, P * c:P * c + P], x_in[:, t, P * c:P * c + P], ident[:])
                    last.then_inc(S["xT_done"], 1)
                if name == "qk":
                    i = QK_SLOT[s]
                    start = QK + (i % 2) * D + (i // 2) * P
                    if i == 0:
                        wait(pe, S["xlo_done"], 4 * b1 + 4)
                        wait(pe, S["xhi_done"], 4 * b1 + 4)
                    split_matmul(p_front[:, :], weights(start, P), x_row(par1), "qk_done")
                if name == "v":
                    split_matmul(p_front[:, 0:D + E], x_tile(par1, s - 9), weights(VG, D + E), "v_done")
                if name == "latent":
                    split_matmul(p_front[:, :], weights(DD, 2 * L), x_row(par1), "latent_done")
                if name == "gateT":
                    wait(pe, S["cparts_done"], 2 * (b1 + 1))
                    for t in range(TILES):
                        last = pe.transpose(p_front[0:4 * E, P * t:P * t + P],
                                            c_parts[:, t, :, :].rearrange("p r e -> p (r e)"), ident[:])
                    last.then_inc(S["gateT_done"], 1)

            def mla_early(b, t, j, body):
                tile = 4 * b + t
                if j == 1:
                    wait(pe, S["mo_out"], tile - 1)
                    wait(pe, S["mkv_out"], tile + 1 if body else TILES * B)
                    for c in range(CH):
                        last = pe.transpose(p_mla[:, P * c:P * c + P], mo[:, P * c:P * c + P], ident[:])
                    last.then_inc(S["moT_done"], 1)
                if j == 2:
                    wait(pe, S["molo_done"], tile - 1)
                    wait(pe, S["mohi_done"], tile - 1)
                    split_matmul(p_mla[:, 0:D], lambda c: (moT_hi[:, c, :], moT_lo[:, c, :]), weights(WO, D), "wo_done")

            def values(b, s, par):
                t, j = ((s - 1) // 4) % 4, (s - 1) % 4
                wait(pe, S["exp_done"], 4 * (16 * b + s))
                if s == 1:
                    wait(pe, S["v_out"], 4 * b + 4)
                if j == 0:
                    wait(pe, S["av_out"], 4 * b + t)
                for i in range(GROUP):
                    last = pe.matmul(p_av[32 * i:32 * i + DH + 1, :], v_one[:, par, j, GROUP * t + i, :],
                                     probs[:, (s - 1) % 2, i, :], start=(j == 0), stop=(j == 3))
                last.then_inc(S["av_done"], 1)

            def slot(b, s, par, prev, body, nxt):
                t, j = s // 4, s % 4
                n = 16 * b + s
                tile = 4 * b + t
                there, u, mg, mi = max_unit(b, s, body, nxt)
                early, late = front_bank_users(s, prev, body, nxt)
                if there and mi == 0 and mg in (0, 2):
                    wait(pe, stacked[mg // 2], STACKED * (b + 1 + (1 if mg == 0 else 0)))
                if body:
                    if j == 0:
                        wait(pe, mrows[t % 2], 48 * (2 * b + t // 2 + 1))
                    if s == 0 and isinstance(b, int) and b == 0:
                        pe.wait_ge(S["wlo_done"], len(pieces) + 1)
                    scores_t(b, t, j, s, 0)
                    scores_t(b, t, j, s, 1)
                if there:
                    max_scores(u, mg, mi, 0)
                    max_scores(u, mg, mi, 1)
                if j in (1, 2) and (prev if t <= 1 else body):
                    mla_early(b, t, j, body)
                if prev if s == 0 else body:
                    values(b, s, 1 - par if s == 0 else par)
                if early:
                    front_bank_free(b, s, False, prev, body, nxt)
                    front(b, s, par, early)
                if body:
                    scores_t(b, t, j, s, 2)
                    scores_t(b, t, j, s, 3)
                if j == 0 and body:
                    wait(pe, S["mq_out"], tile + 1)
                    if s == 0:
                        wait(pe, S["lat_lo_done"], b + 1)
                    pe.matmul(p_mla[:, :], latent[:, P * t:P * t + P], up_hi[:], start=True, stop=False)
                    pe.matmul(p_mla[:, :], latent[:, P * t:P * t + P], up_lo[:], start=False, stop=True).then_inc(S["mkv_done"], 1)
                if there:
                    max_scores(u, mg, mi, 2)
                    max_scores(u, mg, mi, 3)
                if body:
                    wait(pe, S["scaled_done"], 2 * n)
                    split_matmul(p_moe[:].rearrange("p e f -> p (e f)"), x_tile(par, t), weights(EX + 512 * j, 512), "moe_done")
                if late:
                    front_bank_free(b, s, True, prev, body, nxt)
                    front(b, s, par, late)
                if j == 3 and (nxt if t == 3 else body):
                    wait(pe, S["s_out"], tile - 1)
                    split_matmul(p_mla[:, 0:D], x_tile(1 - par, 0) if t == 3 else x_tile(par, t + 1), weights(MQ, D), "mq_done")

            pe.wait_ge(S["consts_done"], 1)
            pe.wait_ge(S["wlo_done"], len(pieces) + 1)
            pe.wait_ge(S["eb_ready"], 16)
            pe.wait_ge(S["ones_done"], 1)
            pe.wait_ge(S["av_zeroed"], 1)
            pe.wait_ge(S["vones_done"], 2)
            batches(pe, slot)

        @block.scalar
        def _(act):
            def exponentials(b, s, par, i):
                n = 64 * b + 4 * s + i
                wait(act, S["st_done"], n + 1)
                if i == 0:
                    wait(act, S["av_done"], 16 * b + s - 1)
                act.activation(probs[:, s % 2, i, :], p2[i % 2][:, :], ACT.Exp, scale=SCALE).then_inc(S["exp_done"], 1)

            def front(b, s, par, name):
                b1, par1 = b + 1, 1 - par
                if name == "bias":
                    t = s // 4
                    wait(act, S["bias_done"], 4 * b + t + 1)
                    if s == 0:
                        wait(act, S["g_done"], 4 * (b - 1))
                    act.activation(z[:, par, t, :], p_front[:, 0:D], ACT.Copy).then_inc(S["z_begun"], 1)
                if name == "max":
                    g = (s // 4 + 1) % 4
                    n = 4 * b + s // 4 + 1
                    wait(act, S["maxT_done"], n + 1)
                    wait(act, mrows[g % 2], 48 * (2 * b + (s // 4 + 1) // 2))
                    act.activation(mparts[:, g % 2, 0, :], p_front[0:16, 0:P], ACT.Copy).then_inc(S["m1_done"], 1)
                if name == "xT":
                    t = s - 2
                    wait(act, S["xT_done"], 4 * b1 + t + 1)
                    if t == 0:
                        wait(act, S["moe_done"], 16 * b)
                        wait(act, S["mq_done"], 4 * b)
                    act.activation(xT_hi[:, par1, :, P * t:P * t + P], p_front[:, 0:D].rearrange("p (c n) -> p c n", c=CH),
                                   ACT.Copy).then_inc(S["xhi_done"], 1)
                if name == "qk":
                    i = QK_SLOT[s]
                    n = 4 * b1 + i
                    wait(act, S["qk_done"], n + 1)
                    if i >= 2:
                        wait(act, stacked[0], STACKED * (b1 + 1))
                    else:
                        wait(act, stacked[1], STACKED * b1)
                    act.activation(parts[:, i % 2, 0, :], p_front[:, :], ACT.Identity, bias=bqk[:, i:i + 1]).then_inc(S["part1_done"], 1)
                if name == "latent":
                    wait(act, S["latent_done"], b1 + 1)
                    wait(act, S["mkv_done"], 4 * b1)
                    act.activation(latent[:], p_front[:, :], ACT.Identity, bias=bdd[:, 0:1]).then_inc(S["lat_hi_done"], 1)
                if name == "gateT":
                    wait(act, S["gateT_done"], b1 + 1)
                    act.activation(cT[:], p_front[0:4 * E, :], ACT.Copy).then_inc(S["cT_done"], 1)

            def slot(b, s, par, prev, body, nxt):
                t, j = s // 4, s % 4
                n = 16 * b + s
                tile = 4 * b + t
                early, late = front_bank_users(s, prev, body, nxt)
                if body:
                    exponentials(b, s, par, 0)
                    exponentials(b, s, par, 1)
                if nxt and s - 1 in QK_SLOT:
                    i = QK_SLOT[s - 1]
                    wait(act, S["rest_done"], 4 * (b + 1) + i + 1)
                    act.activation(parts[:, i % 2, 1, :], rest[:], ACT.Copy).then_inc(S["part2_done"], 1)
                if j == 1 and (prev if t <= 1 else body):
                    wait(act, S["moT_done"], tile - 1)
                    wait(act, S["wo_done"], tile - 2)
                    act.activation(moT_hi[:], p_mla[:, 0:D].rearrange("p (c n) -> p c n", c=CH), ACT.Copy).then_inc(S["mohi_done"], 1)
                if j == 0 and (prev if t == 0 else body):
                    wait(act, S["av_done"], n)
                    wait(act, S["attnT_done"], 4 * b + t - 1)
                    act.activation(av[:], p_av[:, :], ACT.Copy).then_inc(S["av_out"], 1)
                if early:
                    front(b, s, par, early)
                if body:
                    exponentials(b, s, par, 2)
                    exponentials(b, s, par, 3)
                    wait(act, S["moe_done"], n + 1)
                    for k in range(2):
                        e = 2 * j + k
                        wait(act, S["moe_added" if k else "moe_one"], n)
                        act.activation(scaled[:, k, :], p_moe[:, k, :], ACT.Copy,
                                       scale=combine[:, par, t, e:e + 1]).then_inc(S["scaled_done"], 1)
                if late:
                    front(b, s, par, late)
                if j == 3 and body:
                    wait(act, S["mshift_done"], tile + 1)
                    act.activation(msc[:, t % 2], msc[:, t % 2], ACT.Exp, scale=SCALE).then_inc(S["mexp_done"], 1)
                if s == 13 and nxt:
                    wait(act, S["gshift_done"], b + 2)
                    act.activation(gate[:], gshift[:], ACT.Exp).then_inc(S["gexp_done"], 1)
                if prev and 4 <= s <= 7:
                    f = s - 4
                    wait(act, S["z_ready"], b)
                    wait(act, S["res_done"], 4 * (b - 1) + max(f - 1, 0))
                    act.activation(th[:, f % 2, :], z[:, 1 - par, f, :], ACT.Tanh, scale=0.5).then_inc(S["tanh_done"], 1)

            for n, (start, width) in enumerate(pieces):
                two = start in (VG, DD) or EX <= start < WO
                act.wait_ge(w_loaded[n], 32 if two else 16)
                for to, src in weight_views(w_hi, start, width):
                    last = act.activation(to, src, ACT.Copy)
                last.then_inc(S["whi_done"], 1)
            act.wait_ge(w_loaded[-2], 32)
            for to, src in up_views(up_hi[:], up_stage):
                last = act.activation(to, src, ACT.Copy)
            last.then_inc(S["whi_done"], 1)
            act.wait_ge(w_loaded[-1], 64)
            act.activation(eb[:], eb_stage, ACT.Copy).then_inc(S["whi_done"], 1)
            act.wait_ge(S["bias_loaded"], 16 * 11)
            for to, src in up_views(bup_all[:], rest[:]):
                last = act.activation(to, src, ACT.Copy)
            last.then_inc(S["bup_done"], 1)
            batches(act, slot)

        @block.vector
        def _(dve):
            def row_max(u, mg, mi, qt):
                wait(dve, S["max_scores_done"], 4 * u + qt + 1)
                if mi == 0 and qt == 0:
                    wait(dve, S["maxT_done"], front_group(u) - 1)
                dve.tensor_reduce(negmax[:, mg % 2, 4 * mi + qt:4 * mi + qt + 1], p1[qt % 2][:, :], AX, ALU.max,
                                  negate=True).then_inc(S["max_done"], 1)

            def front_group(u):
                return u // 4 if isinstance(u, int) else u_group[0]

            u_group = [0]

            def sum_scores(tile, m, lo):
                wait(dve, S["score_products"], 2 * tile + lo + 1)
                if lo == 0:
                    wait(dve, S["value_products"], 2 * tile - 2)
                dve.tensor_reduce(msc[:, m, 8 * lo:8 * lo + 8, :].rearrange("p h g -> p (h g)"),
                                  prod[:, 1 - lo, :].rearrange("p (a d) -> p a d", d=DH), AX, ALU.add).then_inc(S["scores_reduced"], 1)

            def sum_values(tile, lo):
                wait(dve, S["value_products"], 2 * tile + lo + 1)
                if lo == 0:
                    wait(dve, S["moT_done"], tile)
                dve.tensor_reduce(mo[:, P * lo:P * lo + P], prod[:, lo, :].rearrange("p (a g) -> p a g", g=H),
                                  AX, ALU.add).then_inc(S["values_reduced"], 1)

            def front(b, s, par, name):
                b1, par1 = b + 1, 1 - par
                if name == "attn":
                    n = 4 * b + s // 4
                    g = (s // 4 - 1) % 4
                    wait(dve, S["attnT_done"], n)
                    o4 = p_front[:, :].rearrange("p (q h r) -> p q h r", q=TILES, h=GROUP)
                    wait(dve, S["attn_out"], n - 1)
                    dve.reciprocal(arec[:], o4[:, :, :, DH]).then_inc(S["arec_done"], 1)
                    wait(dve, S["arec_done"], n)
                    if s == 5:
                        wait(dve, S["z_ready"], b)
                    dve.tensor_tensor(attn[:, :, GROUP * DH * g:GROUP * DH * (g + 1)].rearrange("p q (h d) -> p q h d", h=GROUP),
                                      o4[:, :, :, 0:DH], arec[:].unsqueeze(3).broadcast_to([P, TILES, GROUP, DH]),
                                      ALU.mult).then_inc(S["attn_out"], 1)
                if name == "max":
                    g = (s // 4 + 1) % 4
                    n = 4 * b + s // 4 + 1
                    wait(dve, S["m1_done"], n + 1)
                    wait(dve, S["m3_done"], n)
                    dve.tensor_tensor(mrest[:], p_front[0:16, 0:P], mparts[:, g % 2, 0, :], ALU.subtract).then_inc(S["mrest_done"], 1)
                    wait(dve, S["mrest_done"], n + 1)
                    dve.tensor_copy(mparts[:, g % 2, 1, :], mrest[:]).then_inc(S["m2_done"], 1)
                    wait(dve, S["m2_done"], n + 1)
                    dve.tensor_tensor(mparts[:, g % 2, 2, :], mrest[:], mparts[:, g % 2, 1, :], ALU.subtract).then_inc(S["m3_done"], 1)
                if name == "xT":
                    t = s - 2
                    wait(dve, S["xhi_done"], 4 * b1 + t + 1)
                    at = (slice(None), par1, slice(None), slice(P * t, P * t + P))
                    dve.tensor_tensor(xT_lo[at], p_front[:, 0:D].rearrange("p (c n) -> p c n", c=CH), xT_hi[at].bitcast(F32),
                                      ALU.subtract).then_inc(S["xlo_done"], 1)
                if name == "qk":
                    i = QK_SLOT[s]
                    n = 4 * b1 + i
                    wait(dve, S["part1_done"], n + 1)
                    wait(dve, S["part3_done"], n)
                    dve.scalar_tensor_tensor(out=rest[:], in0=p_front[:, :], scalar=bqk[:, i:i + 1], in1=parts[:, i % 2, 0, :],
                                             op0=ALU.add, op1=ALU.subtract).then_inc(S["rest_done"], 1)
                if name == "v":
                    t = s - 9
                    wait(dve, S["v_done"], 4 * b1 + t + 1)
                    if t == 0:
                        wait(dve, S["av_done"], 16 * b)
                        wait(dve, S["gshift_done"], b1)
                    dve.tensor_tensor(v_one[:, par1, t, :, 0:DH], p_front[:, 0:D].rearrange("p (h d) -> p h d", h=H),
                                      bvg_all[:, 0:D].rearrange("p (h d) -> p h d", h=H), ALU.add).then_inc(S["v_out"], 1)
                    dve.tensor_tensor(logits[:, t, :], p_front[:, D:D + E], bvg_all[:, D:D + E], ALU.add).then_inc(S["logits_out"], 1)
                if name == "latent":
                    wait(dve, S["lat_hi_done"], b1 + 1)
                    dve.scalar_tensor_tensor(out=latent[L:P, :], in0=p_front[L:P, :], scalar=bdd[L:P, 0:1],
                                             in1=latent[L:P, :].bitcast(F32), op0=ALU.add, op1=ALU.subtract).then_inc(S["lat_lo_done"], 1)

            def gate_softmax(b1):
                wait(dve, S["logits_out"], 4 * b1 + 4)
                dve.tensor_reduce(gsum[:], logits[:], AX, ALU.max).then_inc(S["gmax_done"], 1)
                wait(dve, S["gmax_done"], b1 + 1)
                wait(dve, S["combine_done"], b1)
                dve.tensor_tensor(gshift[:], logits[:], gsum[:].unsqueeze(2).broadcast_to([P, TILES, E]), ALU.subtract).then_inc(S["gshift_done"], 1)

            def gate_top(b, b1, par1):
                wait(dve, S["gexp_done"], b1 + 1)
                dve.tensor_reduce(gsum[:], gate[:], AX, ALU.add).then_inc(S["gsum_done"], 1)
                wait(dve, S["gsum_done"], b1 + 1)
                dve.reciprocal(gsum[:], gsum[:]).then_inc(S["grec_done"], 1)
                wait(dve, S["grec_done"], b1 + 1)
                dve.tensor_tensor(gate[:], gate[:], gsum[:].unsqueeze(2).broadcast_to([P, TILES, E]), ALU.mult).then_inc(S["gate_done"], 1)
                wait_apart(dve, S["dve_passed"], S["gate_done"], b1 + 1)
                for t in range(TILES):
                    dve.max(top[:, t, :], gate[:, t, :]).then_inc(S["top_done"], 1)
                for t in range(TILES):
                    wait_apart(dve, S["dve_passed"], S["top_done"], 4 * b1 + t + 1)
                    dve.max_index(topi[:, t, :], top[:, t, :], gate[:, t, :]).then_inc(S["topi_done"], 1)
                wait(dve, S["topi_done"], 4 * b1 + 4)
                dve.tensor_copy(topf[:], topi[:, :, 0:2]).then_inc(S["topf_done"], 1)
                wait(dve, S["topf_done"], b1 + 1)
                for k in range(2):
                    dve.tensor_tensor(pick[:, k, :, :], iota[:], topf[:, :, k:k + 1].broadcast_to([P, TILES, E]), ALU.is_equal).then_inc(S["pick_done"], 1)
                wait(dve, S["pick_done"], 2 * (b1 + 1))
                dve.tensor_tensor(pick[:, 0, :, :], pick[:, 0, :, :], pick[:, 1, :, :], ALU.add).then_inc(S["picks_done"], 1)
                wait(dve, S["picks_done"], b1 + 1)
                wait(dve, S["scaled_done"], 32 * b)
                dve.tensor_tensor(combine[:, par1, :, :], gate[:], pick[:, 0, :, :], ALU.mult).then_inc(S["combine_done"], 1)
                wait(dve, S["combine_done"], b1 + 1)
                wait(dve, S["gateT_done"], b1)
                dve.tensor_copy(c_hi[:], combine[:, par1, :, :]).then_inc(S["chi_done"], 1)
                wait(dve, S["chi_done"], b1 + 1)
                both = [P, TILES, 2, E]
                dve.tensor_copy(c_parts[:, :, 0::2, :], c_hi[:].bitcast(F32).unsqueeze(2).broadcast_to(both)).then_inc(S["cparts_done"], 1)
                dve.tensor_tensor(c_parts[:, :, 1::2, :], combine[:, par1, :, :].unsqueeze(2).broadcast_to(both),
                                  c_hi[:].bitcast(F32).unsqueeze(2).broadcast_to(both), ALU.subtract).then_inc(S["cparts_done"], 1)

            def slot(b, s, par, prev, body, nxt):
                t, j = s // 4, s % 4
                tile = 4 * b + t
                two_before = prev if t <= 1 else body
                b1, par1 = b + 1, 1 - par
                there, u, mg, mi = max_unit(b, s, body, nxt)
                u_group[0] = 4 * b + (s + 6) // 4
                early, late = front_bank_users(s, prev, body, nxt)
                if there:
                    row_max(u, mg, mi, 0)
                    row_max(u, mg, mi, 1)
                if early:
                    front(b, s, par, early)
                if j == 0 and body:
                    wait(dve, S["mq_done"], tile + 1)
                    wait(dve, S["score_products"], 2 * tile)
                    dve.tensor_tensor(mq[:], p_mla[:, 0:D], bq_all[:], ALU.add).then_inc(S["mq_out"], 1)
                if j == 0 and (prev if t == 0 else body):
                    wait(dve, S["mexp_done"], tile)
                    dve.tensor_reduce(msum[:], msc[:, (t - 1) % 2], AX, ALU.add).then_inc(S["msum_done"], 1)
                if j == 0 and two_before:
                    sum_values(tile - 2, 1)
                if j == 0 and (prev if t == 0 else body):
                    wait(dve, S["msum_done"], tile)
                    wait(dve, S["mo_out"], tile - 2)
                    dve.reciprocal(mrec[:, (t - 1) % 2, :], msum[:]).then_inc(S["mrec_done"], 1)
                if j == 0 and two_before:
                    wait(dve, S["values_reduced"], 2 * tile - 2)
                    wait(dve, S["mrec_done"], tile - 1)
                    dve.tensor_tensor(mo[:].rearrange("p (h d) -> p h d", h=H), mo[:].rearrange("p (h d) -> p h d", h=H),
                                      mrec[:, t % 2, :].unsqueeze(2).broadcast_to([P, H, DH]), ALU.mult).then_inc(S["mo_out"], 1)
                if j == 1 and two_before:
                    wait(dve, S["mohi_done"], tile - 1)
                    wait(dve, S["wo_done"], tile - 2)
                    dve.tensor_tensor(moT_lo[:], p_mla[:, 0:D].rearrange("p (c n) -> p c n", c=CH), moT_hi[:].bitcast(F32),
                                      ALU.subtract).then_inc(S["molo_done"], 1)
                if j == 1 and (prev if t == 0 else body):
                    sum_values(tile - 1, 0)
                if j == 2 and body:
                    sum_scores(tile, t % 2, 0)
                if j == 3 and body:
                    sum_scores(tile, t % 2, 1)
                    wait(dve, S["scores_reduced"], 2 * tile + 2)
                    dve.tensor_reduce(mmax[:], msc[:, t % 2], AX, ALU.max).then_inc(S["mmax_done"], 1)
                    wait(dve, S["mmax_done"], tile + 1)
                    dve.tensor_tensor(msc[:, t % 2], msc[:, t % 2], mmax[:].unsqueeze(2).broadcast_to([P, H, H]), ALU.subtract).then_inc(S["mshift_done"], 1)
                if there:
                    row_max(u, mg, mi, 2)
                    row_max(u, mg, mi, 3)
                if late:
                    front(b, s, par, late)
                if nxt and 1 <= s <= 4:
                    k = s - 1
                    if k == 0:
                        wait(dve, S["rstd_done"], b1 + 1)
                    dve.tensor_scalar(x_in[:, k, :], x_in[:, k, :], meanvar[:, k, 0:1], rstd[:, k:k + 1],
                                      ALU.subtract, ALU.mult).then_inc(S["xn_done"], 1)
                if nxt and s == 0:
                    wait(dve, S["x_loaded"], 16 * (b1 + 1))
                    for k in range(TILES):
                        dve.bn_stats(stats[:, k, :], x_in[:, k, :]).then_inc(S["stats_done"], 1)
                    wait(dve, S["stats_done"], 4 * (b1 + 1))
                    wait_apart(dve, S["dve_passed"], S["xn_done"], 4 * b1)
                    wait_apart(dve, S["dve_passed"], S["ve_done"], b1)
                    for k in range(TILES):
                        dve.bn_aggr(meanvar[:, k, :], stats[:, k, :]).then_inc(S["meanvar_done"], 1)
                if j == 0 and body:
                    wait(dve, S["mkv_done"], tile + 1)
                    wait(dve, S["value_products"], 2 * tile - 2)
                    dve.tensor_tensor(mkv[:, t % 2].rearrange("p r n -> p (r n)"), p_mla[:, :], bup_all[:], ALU.add).then_inc(S["mkv_out"], 1)
                if j == 2 and two_before:
                    wait(dve, S["wo_done"], tile - 1)
                    if t >= 2:
                        wait(dve, S["w_done"], tile - 5)
                    else:
                        wait(dve, S["w_done"], 4 * (b - 1))
                    dve.tensor_tensor(s_mla[:, (t - 2) % 4, :], p_mla[:, 0:D], bout_all[:], ALU.add).then_inc(S["s_out"], 1)
                if s == 13 and nxt:
                    gate_softmax(b1)
                if s == 14 and nxt:
                    gate_top(b, b1, par1)
                if prev and 4 <= s <= 7:
                    f = s - 4
                    n = 4 * (b - 1) + f
                    wait(dve, S["tanh_done"], n + 1)
                    dve.scalar_tensor_tensor(out=th[:, f % 2, :], in0=th[:, f % 2, :], scalar=1.0, in1=z[:, 1 - par, f, :],
                                             op0=ALU.add, op1=ALU.mult).then_inc(S["g_done"], 1)
                    wait(dve, S["g_done"], n + 1)
                    wait(dve, S["s_out"], n + 1)
                    dve.scalar_tensor_tensor(out=th[:, f % 2, :], in0=th[:, f % 2, :], scalar=0.5, in1=s_mla[:, f, :],
                                             op0=ALU.mult, op1=ALU.mult).then_inc(S["w_done"], 1)

            dve.memset(p_av[:, :], 0.0).then_inc(S["av_zeroed"], 1)
            for n, (start, width) in enumerate(pieces):
                dve.wait_ge(S["whi_done"], n + 1)
                for (to, src), (high, _) in zip(weight_views(w_lo, start, width), weight_views(w_hi, start, width)):
                    last = dve.tensor_tensor(to, src, high.bitcast(F32), ALU.subtract)
                last.then_inc(S["wlo_done"], 1)
            dve.wait_ge(S["whi_done"], len(pieces) + 1)
            for (to, src), (high, _) in zip(up_views(up_lo[:], up_stage), up_views(up_hi[:], up_stage)):
                last = dve.tensor_tensor(to, src, high.bitcast(F32), ALU.subtract)
            last.then_inc(S["wlo_done"], 1)
            dve.wait_ge(S["whi_done"], len(pieces) + 2)
            dve.tensor_tensor(eb_low, eb_stage, eb[:].bitcast(F32), ALU.subtract).then_inc(S["eblo_done"], 1)
            dve.wait_ge(S["bias_loaded"], 16 * 11)
            dve.wait_ge(S["bup_done"], 1)
            dve.wait_ge(S["iota_done"], 1)
            batches(dve, slot)

        @block.gpsimd
        def _(pool):
            def score_product(tile, m, lo):
                heads = slice(8 * lo, 8 * lo + 8)
                shape = [P, 8, H, H]
                if lo == 0:
                    wait(pool, S["mkv_out"], tile + 1)
                wait(pool, S["values_reduced"], 2 * tile - 2 + lo)
                pool.tensor_tensor(prod[:, 1 - lo, :].rearrange("p (h g d) -> p h g d", h=8, g=H),
                                   mq[:].rearrange("p (h d) -> p h d", h=H)[:, heads, :].unsqueeze(2).broadcast_to(shape),
                                   mkv[:, m, 0, :].rearrange("p (g d) -> p g d", g=H).unsqueeze(1).broadcast_to(shape),
                                   ALU.mult).then_inc(S["score_products"], 1)

            def value_product(tile, m, lo, body):
                heads = slice(8 * lo, 8 * lo + 8)
                shape = [P, 8, H, H]
                if lo == 0:
                    wait(pool, S["mexp_done"], tile + 1)
                if lo == 0 or body:
                    wait(pool, S["scores_reduced"], 2 * tile + 2 + lo)
                else:
                    wait(pool, S["values_reduced"], 2 * tile)
                pool.tensor_tensor(prod[:, lo, :].rearrange("p (h d g) -> p h d g", h=8, d=H),
                                   msc[:, m, heads, :].unsqueeze(2).broadcast_to(shape),
                                   mkv[:, m, 1, :].rearrange("p (d g) -> p d g", d=DH).unsqueeze(1).broadcast_to(shape),
                                   ALU.mult).then_inc(S["value_products"], 1)

            def add_experts(n, tile, z_tile, first):
                if first:
                    wait(pool, S["z_begun"], tile + 1)
                wait(pool, S["scaled_done"], 2 * n + 2)
                wait(pool, S["moe_added"], n)
                pool.tensor_tensor(z_tile, z_tile, scaled[:, 0, :], ALU.add).then_inc(S["moe_one"], 1)
                wait(pool, S["moe_one"], n + 1)
                pool.tensor_tensor(z_tile, z_tile, scaled[:, 1, :], ALU.add).then_inc(S["moe_added"], 1)

            def slot(b, s, par, prev, body, nxt):
                t, j = s // 4, s % 4
                tile = 4 * b + t
                n = 16 * b + s
                before = prev if t == 0 else body
                b1 = b + 1
                if prev if s == 0 else body:
                    add_experts(n - 1, tile - (1 if j == 0 else 0), z[:, 1 - par, 3, :] if s == 0 else z[:, par, (s - 1) // 4, :], j == 1)
                if nxt and s == 1:
                    wait(pool, S["meanvar_done"], 4 * (b1 + 1))
                    wait_apart(pool, S["pool_passed"], S["rstd_done"], b1)
                    pool.tensor_scalar(vareps[:], meanvar[:, :, 1], EPS, None, ALU.add).then_inc(S["ve_done"], 1)
                    wait(pool, S["ve_done"], b1 + 1)
                    wait(pool, S["xn_done"], 4 * b1)
                    pool.tensor_tensor(rstd[:], vareps[:], half[:], ALU.pow).then_inc(S["rstd_done"], 1)
                if nxt and s - 1 in QK_SLOT:
                    i = QK_SLOT[s - 1]
                    wait(pool, S["part2_done"], 4 * b1 + i + 1)
                    pool.tensor_tensor(parts[:, i % 2, 2, :], rest[:], parts[:, i % 2, 1, :], ALU.subtract).then_inc(S["part3_done"], 1)
                if j == 0 and before:
                    value_product(tile - 1, (t - 1) % 2, 0, body)
                if j in (1, 2) and body:
                    score_product(tile, t % 2, j - 1)
                if j == 3 and before:
                    value_product(tile - 1, (t - 1) % 2, 1, body)
                if prev and s == 2:
                    wait(pool, S["attn_out"], 4 * b)
                    wait(pool, S["moe_added"], 16 * b)
                    pool.tensor_tensor(z[:, 1 - par], z[:, 1 - par], attn[:], ALU.add).then_inc(S["z_ready"], 1)
                if prev and 4 <= s <= 7:
                    f = s - 4
                    wait(pool, S["w_done"], 4 * (b - 1) + f + 1)
                    wait(pool, xfin_loaded[f % 2], 16 * (2 * (b - 1) + f // 2 + 1))
                    pool.tensor_tensor(x_fin[:, f % 2, :], th[:, f % 2, :], x_fin[:, f % 2, :], ALU.add).then_inc(S["res_done"], 1)

            pool.memset(ident[:], 0.0).then_inc(S["ident_zeroed"], 1)
            pool.wait_ge(S["ident_zeroed"], 1)
            pool.affine_select(out=ident[:], in_=ident[:], compare_op=ALU.not_equal, fill=1.0, base=0,
                               pattern=[[-1, P]], channel_multiplier=1).then_inc(S["consts_done"], 1)
            pool.memset(half[:], -0.5).then_inc(S["half_done"], 1)
            pool.iota(iota[:], pattern=[[0, TILES], [1, E]], base=0, channel_multiplier=0,
                      allow_small_or_imprecise_dtypes=True).then_inc(S["iota_done"], 1)
            for p in range(2):
                pool.memset(v_one[:, p, :, :, DH:DH + 1], 1.0).then_inc(S["vones_done"], 1)
            pool.wait_ge(S["vones_done"], 2)
            pool.memset(k_stack[PRODUCTS * DH:ROWS, :, :], 1.0).then_inc(S["ones_done"], 1)
            pool.wait_ge(S["ones_done"], 1)
            pool.wait_ge(S["half_done"], 1)
            batches(pool, slot)


_INS = ["L0_attn_x", "L0_attn_Wq", "L0_attn_bq", "L0_attn_Wdown", "L0_attn_bdown", "L0_attn_Wup", "L0_attn_bup", "L0_attn_Wout",
        "L0_attn_bout", "L0_ffn_W_qkv", "L0_ffn_b_qkv", "L0_ffn_W_gate", "L0_ffn_b_gate", "L0_ffn_W_experts", "L0_ffn_b_experts"]


def kernel(**inputs):
    import numpy as np
    import concourse.bacc as bacc
    from concourse import mybir as m
    from concourse.bass_utils import run_bass_kernel_spmd

    nc = bacc.Bacc("TRN2", target_bir_lowering=False, num_devices=1)
    arrays, args = {}, []
    for name in _INS:
        a = np.ascontiguousarray(inputs[name])
        arrays[f"in_{name}"] = a
        args.append(nc.dram_tensor(f"in_{name}", a.shape, m.dt.from_np(a.dtype), kind="ExternalInput").ap())
    out = nc.dram_tensor("out", inputs["L0_attn_x"].shape, m.dt.float32, kind="ExternalOutput").ap()
    build(nc, *args, out)
    return run_bass_kernel_spmd(nc, [arrays], core_ids=[0]).results[0]["out"]
```

```python
from contextlib import ExitStack

import concourse.bass as bass
from concourse import mybir

ALU = mybir.AluOpType
ACT = mybir.ActivationFunctionType
AX = mybir.AxisListType.X
F32 = mybir.dt.float32
F32R = mybir.dt.float32r
BF16 = mybir.dt.bfloat16
U32 = mybir.dt.uint32

P = 128
EPS = 1e-5
SLOTS = 16
GROUP = 4
PRODUCTS = 6
Q_PARTS = (0, 0, 1, 1, 0, 2)
K_PARTS = (0, 1, 0, 1, 2, 0)
STACK_DMAS = 2 * PRODUCTS
V_SLOT = 8
LATE_VALUES = (2, 3, 5, 14, 15)
END_SLOTS = (4, 8, 10, 11)
LAST_END_SLOTS = (2, 3, 4, 7)
QK_SLOT = {6: 0, 7: 1, 12: 2, 13: 3}


def wait(engine, semaphore, count):
    if not isinstance(count, int) or count > 0:
        engine.wait_ge(semaphore, count)


def wait_apart(engine, passed, semaphore, count):
    wait(engine, semaphore, count)
    if not isinstance(count, int):
        engine.sem_inc(passed, 1)


def end_slots(body):
    return END_SLOTS if body else LAST_END_SLOTS


def front_bank_users(s, prev, body, nxt):
    early = late = None
    if s % 4 == 1 and (prev if s == 1 else body):
        early = "attn"
    if s % 4 == 2 and (nxt if s == 14 else body):
        early = "max"
    if nxt:
        if s == 15:
            early = "latent"
        late = {2: "xT", 3: "xT", 4: "xT", 5: "xT", 6: "qk", 7: "qk", 8: "v", 9: "v", 10: "v", 11: "v",
                12: "qk", 13: "qk"}.get(s)
    if s == 1 and body:
        late = "gateT"
    return early, late


def build(nc, x, Wq, bq, Wdown, bdown, Wup, bup, Wout, bout, W_qkv, b_qkv, W_gate, b_gate, W_experts, b_experts, out):
    B, T, D = x.shape
    E = W_gate.shape[1]
    L = Wdown.shape[1]
    H = 16
    DH = D // H
    TILES = T // P
    CH = D // P
    HC = H // CH
    assert (TILES, CH, H, E, 2 * L, GROUP) == (4, 2, 16, 8, P, 4) and B % 2 == 0
    ROWS = PRODUCTS * DH + 3
    SCALE = float(DH) ** -0.5
    HALF = H * H * DH // 2
    STACKED = 16 * STACK_DMAS

    QK, VG, DD, MQ, EX, WO = 0, 512, 776, 904, 1160, 3208
    NW = WO + D
    pieces = [(QK, 512), (VG, D + E), (DD, 2 * L), (MQ, D)] + [(EX + 512 * e, 512) for e in range(E // 2)] + [(WO, D)]
    UP, EB, BIAS = len(pieces), len(pieces) + 1, len(pieces) + 2
    SPLITS = {0: (0,), 5: (BIAS,), 7: (1,), 8: (2, 3, 4, 5, 6, 7), 10: (8,), 11: (UP, EB)}
    SPLIT_ORDER = [n for ns in SPLITS.values() for n in ns]
    BQ, BUP, BVG, BOUT = 0, D, 3 * D, 4 * D + E
    NB = BOUT + D

    with ExitStack() as ctx:
        def sb(name, shape, dt=F32):
            return ctx.enter_context(nc.sbuf_tensor(name, shape, dt))

        def bank(name, shape):
            return ctx.enter_context(nc.psum_tensor(name, shape, F32))

        def sem(name):
            return ctx.enter_context(nc.semaphore(name))

        w_hi = sb("w_hi", [P, CH, NW], F32R)
        w_lo = sb("w_lo", [P, CH, NW], F32R)
        up_hi = sb("up_hi", [P, 2 * D], F32R)
        up_lo = sb("up_lo", [P, 2 * D], F32R)
        rows = sb("rows", [4 * E + 2, NB + P], F32R)
        eb = rows[0:4 * E, 0:D]
        cT = rows[0:4 * E, D:D + T]
        bias = rows[4 * E:4 * E + 2, 0:NB]
        ones = rows[4 * E:4 * E + 2, NB:NB + P]
        scratch = sb("scratch", [P, 8192])
        stage = scratch[:, 0:CH * NW].rearrange("p (c n) -> p c n", c=CH)
        up_stage = scratch[:, CH * NW:CH * NW + 2 * D]
        eb_stage = scratch[0:4 * E, CH * NW + 2 * D:CH * NW + 3 * D]
        eb_low = scratch[0:4 * E, CH * NW + 3 * D:CH * NW + 4 * D].bitcast(F32R)
        probs = scratch[:, 0:4096].rearrange("p (s i q) -> p s i q", s=2, i=GROUP)
        prod = scratch[:, 4096:8192].rearrange("p (s n) -> p s n", s=2)
        assert CH * NW + 4 * D <= 8192
        ident = sb("ident", [P, P])
        iota = sb("iota", [P, TILES, E])
        half = sb("half", [P, TILES])
        bqk = sb("bqk", [P, 4])
        bdd = sb("bdd", [P, 1])

        x_in = sb("x_in", [P, TILES, D])
        shift = sb("shift", [P, 2, TILES])
        x_fin = sb("x_fin", [P, 2, D])
        stats = sb("stats", [P, TILES, 6])
        meanvar = sb("meanvar", [P, TILES, 2])
        vareps = sb("vareps", [P, TILES])
        rstd = sb("rstd", [P, TILES])
        xT_hi = sb("xT_hi", [P, 2, CH, T], F32R)
        xT_lo = sb("xT_lo", [P, 2, CH, T], F32R)
        parts = sb("parts", [P, 2, 3, T], BF16)
        rest = sb("rest", [P, T])
        q_stack = sb("q_stack", [ROWS, H, T], BF16)
        k_stack = sb("k_stack", [ROWS, H, T], BF16)
        v_one = sb("v_one", [P, 2, TILES, H, DH + 1])
        logits = sb("logits", [P, TILES, E])
        gsum = sb("gsum", [P, TILES])
        gshift = sb("gshift", [P, TILES, E])
        gate = sb("gate", [P, TILES, E])
        top = sb("top", [P, TILES, 8])
        topi = sb("topi", [P, TILES, 8], U32)
        topf = sb("topf", [P, TILES, 2])
        pick = sb("pick", [P, 2, TILES, E])
        combine = sb("combine", [P, 2, TILES, E])
        c_hi = sb("c_hi", [P, TILES, E], F32R)
        c_parts = sb("c_parts", [P, TILES, 4, E])
        latent = sb("latent", [P, T], F32R)

        negmax = sb("negmax", [P, 2, 16])
        mrest = sb("mrest", [16, P])
        mparts = sb("mparts", [16, 2, 3, P], BF16)
        av = sb("av", [P, T])
        arec = sb("arec", [P, TILES, GROUP])
        attn = sb("attn", [P, TILES, D])
        scaled = sb("scaled", [P, 2, 2, D])
        acc = sb("acc", [P, 2, 2, D])
        z = sb("z", [P, TILES, D])

        mq = sb("mq", [P, D])
        mkv = sb("mkv", [P, 2, 2, D])
        msc = sb("msc", [P, 2, H, H])
        mmax = sb("mmax", [P, H])
        msum = sb("msum", [P, H])
        mrec = sb("mrec", [P, 2, H])
        mo = sb("mo", [P, D])
        moT_hi = sb("moT_hi", [P, CH, P], F32R)
        moT_lo = sb("moT_lo", [P, CH, P], F32R)
        s_mla = sb("s_mla", [P, TILES, D])
        th = sb("th", [P, 2, D])

        bias_stage = q_stack[4 * E:4 * E + 2].rearrange("r h t -> r (h t)")[:, 2 * NB:4 * NB].bitcast(F32)
        bias_low = q_stack[4 * E:4 * E + 2].rearrange("r h t -> r (h t)")[:, 0:2 * NB].bitcast(F32R)

        p1 = [bank(f"p1_{i}", [P, T]) for i in range(2)]
        p2 = [bank(f"p2_{i}", [P, T]) for i in range(2)]
        p_av = bank("p_av", [P, T])
        p_moe = bank("p_moe", [P, 2, D])
        p_mla = bank("p_mla", [P, 2 * D])
        p_front = bank("p_front", [P, T])

        names = """st_done max_scores_done av_done moe_done mq_done mkv_done moT_done wo_done xT_done qk_done v_done latent_done
            gateT_done bias_done maxT_done attnT_done
            exp_done part1_done part2_done xhi_done lat_hi_done gexp_done cT_done mexp_done mohi_done m1_done
            av_out tanh_done scaled_done whi_done
            max_done stats_done meanvar_done xn_done xlo_done rest_done v_out logits_out gmax_done gshift_done gsum_done grec_done
            gate_done top_done topi_done topf_done pick_done picks_done combine_done chi_done cparts_done
            lat_lo_done mrest_done m2_done m3_done arec_done attn_out mq_out mkv_out scores_reduced values_reduced mmax_done mshift_done msum_done
            mrec_done mo_out molo_done s_out g_done w_done wlo_done bias_ready ones_out av_zeroed
            score_products value_products z_half z_merged moe_added ve_done rstd_done neg_done shift_done part3_done z_ready res_done consts_done ident_zeroed iota_done half_done ones_done
            x_loaded dve_passed pool_passed sp_passed vones_done eb_ready bias_loaded""".split()
        S = {n: sem(n) for n in names}
        w_loaded = [sem(f"w_loaded{n}") for n in range(len(pieces) + 3)]
        stacked = [sem("stacked0"), sem("stacked1")]
        mrows = [sem("mrows0"), sem("mrows1")]
        xfin_loaded = [sem("xfin_loaded0"), sem("xfin_loaded1")]
        stored = [sem("stored0"), sem("stored1")]

        x_v = x.rearrange("b (t p) d -> b p t d", p=P)
        out_v = out.rearrange("b (t p) d -> b p t d", p=P)

        block = ctx.enter_context(nc.Block())

        def weight_views(w, start, width):
            if start != QK:
                return [(w[:, :, start:start + width], stage[:, :, start:start + width])]
            return [(w[:, c, QK:QK + width].rearrange("p (k d h) -> p k d h", d=DH, h=HC),
                     stage[:, c, QK:QK + width].rearrange("p (k h d) -> p k d h", d=DH, h=HC)) for c in range(CH)]

        def up_views(to, src):
            src = src.rearrange("p (h r d) -> p r h d", r=2, d=DH)
            return [(to[:, 0:D].rearrange("p (h d) -> p h d", h=H), src[:, 0]),
                    (to[:, D:2 * D].rearrange("p (d h) -> p h d", h=H), src[:, 1])]

        def bias_views(to, src):
            return ([(to[:, BQ:BUP], src[:, BQ:BUP]), (to[:, BVG:NB], src[:, BVG:NB])]
                    + up_views(to[:, BUP:BVG], src[:, BUP:BVG]))

        def split_views(n, w, up, experts_bias, biases):
            if n == UP:
                return up_views(up, up_stage)
            if n == EB:
                return [(experts_bias, eb_stage)]
            if n == BIAS:
                return bias_views(biases, bias_stage)
            return weight_views(w, *pieces[n])

        def batches(engine, slot):
            for s in range(SLOTS):
                slot(-1, s, 1, False, False, True)
            for s in range(SLOTS):
                slot(0, s, 0, False, True, True)
            with engine.Fori(0, (B - 2) // 2) as i:
                for par in (1, 0):
                    for s in range(SLOTS):
                        slot(2 * i + (1 if par else 2), s, par, True, True, True)
            for s in range(SLOTS):
                slot(B - 1, s, 1, True, True, False)
            for s in range(max(LAST_END_SLOTS) + 2):
                slot(B, s, 0, True, False, False)

        def max_unit(b, s, body, nxt):
            there = body if s <= 9 else nxt
            return there, 16 * b + s + 6, ((s + 6) // 4) % 4, (s + 2) % 4

        @block.sync
        def _(sp):
            def sp_wait(semaphore, count):
                wait_apart(sp, S["sp_passed"], semaphore, count)

            def load_weights():
                sp.dma_start(x_in[:], x_v[0]).then_inc(S["x_loaded"], 16)
                for n, (start, width) in enumerate(pieces):
                    to = stage[:, :, start:start + width]
                    if start == QK:
                        srcs = [(to, W_qkv[:, 0:512])]
                    elif start == VG:
                        srcs = [(to[:, :, 0:D], W_qkv[:, 2 * D:3 * D]), (to[:, :, D:D + E], W_gate)]
                    elif start == DD:
                        srcs = [(to[:, :, 0:L], Wdown), (to[:, :, L:2 * L], Wdown)]
                    elif start == MQ:
                        srcs = [(to, Wq)]
                    elif start == WO:
                        srcs = [(to, Wout)]
                    else:
                        e = (start - EX) // D
                        srcs = [(to[:, :, 0:D], W_experts[e]), (to[:, :, D:2 * D], W_experts[e + 1])]
                    for dst, src in srcs:
                        sp.dma_start(dst, src.rearrange("(c p) n -> p c n", p=P)).then_inc(w_loaded[n], 16)
                    if start == QK:
                        for i in range(4):
                            src = b_qkv[(i % 2) * D + (i // 2) * P:][0:P].rearrange("(h d) -> d h", h=HC)
                            sp.dma_start(bqk[:, i:i + 1], src, allow_slow_non_contiguous=True).then_inc(S["bias_loaded"], 16)
                        for r in range(2):
                            sp.dma_start(bdd[L * r:L * r + L, :], bdown.rearrange("(a n) -> n a", a=1), allow_slow_non_contiguous=True).then_inc(S["bias_loaded"], 16)
                        for start_b, src in ((BQ, bq), (BUP, bup), (BVG, b_qkv[2 * D:3 * D]), (BVG + D, b_gate), (BOUT, bout)):
                            width_b = src.shape[0]
                            sp.dma_start(bias_stage[:, start_b:start_b + width_b],
                                         src.rearrange("(a n) -> a n", a=1).broadcast_to([2, width_b])).then_inc(w_loaded[BIAS], 16)
                for r in range(2):
                    sp.dma_start(up_stage[L * r:L * r + L, :], Wup).then_inc(w_loaded[UP], 16)
                for r in range(4):
                    sp.dma_start(eb_stage[E * r:E * r + E, :], b_experts).then_inc(w_loaded[EB], 16)

            def stack(c, b):
                sp_wait(S["part2_done"], 4 * b + 2 * c + 2)
                sp_wait(S["st_done"], 64 * b - (32 if c == 0 else 0))
                heads = slice(HC * c, HC * c + HC)
                copies = ([(q_stack, r, 0, part) for r, part in enumerate(Q_PARTS)]
                          + [(k_stack, r, 1, part) for r, part in enumerate(K_PARTS)])
                for third in (False, True):
                    if third:
                        sp_wait(S["part3_done"], 4 * b + 2 * c + 2)
                    for to, r, which, part in copies:
                        if (part == 2) == third:
                            sp.dma_start(to[DH * r:DH * r + DH, heads, :], parts[:, which, part, :]).then_inc(stacked[c], 16)

            def slot(b, s, par, prev, body, nxt):
                if isinstance(b, int) and b == -1 and s == 7:
                    sp.wait_ge(S["wlo_done"], SPLIT_ORDER.index(BIAS) + 1)
                    sp.dma_start(bias[1:2, :].bitcast(F32), bias_low[1:2, :].bitcast(F32)).then_inc(S["bias_ready"], 16)
                    sp.wait_ge(S["bias_ready"], 16)
                if isinstance(b, int) and b == -1 and s == 15:
                    sp.wait_ge(S["wlo_done"], SPLIT_ORDER.index(EB) + 1)
                    sp.dma_start(eb[2 * E:4 * E, :].bitcast(F32), eb_low[2 * E:4 * E, :].bitcast(F32)).then_inc(S["eb_ready"], 16)
                if s == 0 and body and nxt:
                    sp_wait(S["xT_done"], 4 * (b + 1))
                    sp.dma_start(x_in[:], x_v[b + 1]).then_inc(S["x_loaded"], 16)
                if s == 0 and body:
                    stack(1, b)
                if s == 8 and nxt:
                    stack(0, b + 1)
                if prev and s in end_slots(body):
                    t = end_slots(body).index(s)
                    sp_wait(stored[t % 2], 16 * (2 * (b - 1) + t // 2 + 1))
                    sp.dma_start(x_fin[:, t % 2, :], x_v[b - 1][:, t, :]).then_inc(xfin_loaded[t % 2], 16)
                if s % 4 == 2 and (nxt if s == 14 else body):
                    g = (s // 4 + 1) % 4
                    n = 4 * b + s // 4 + 1
                    sp_wait(S["m3_done"], n + 1)
                    for r in range(3):
                        row = PRODUCTS * DH + r
                        sp.dma_start(q_stack[row:row + 1, GROUP * g:GROUP * g + GROUP, :], mparts[:, g % 2, r, :]).then_inc(mrows[g % 2], 16)
                if prev and s - 1 in end_slots(body):
                    t = end_slots(body).index(s - 1)
                    sp_wait(S["res_done"], 4 * (b - 1) + t + 1)
                    sp.dma_start(out_v[b - 1][:, t, :], x_fin[:, t % 2, :]).then_inc(stored[t % 2], 16)

            for p in range(2):
                sp.sem_inc(stored[p], 16)
            load_weights()
            batches(sp, slot)
            for p in range(2):
                sp.wait_ge(stored[p], 16 * (2 * B + 1))

        @block.tensor
        def _(pe):
            def front_bank_free(b, s, late, prev, body, nxt):
                at, name = s, front_bank_users(s, prev, body, nxt)[0] if late else None
                while at > 0 and not name:
                    at -= 1
                    name = next((user for user in reversed(front_bank_users(at, prev, body, nxt)) if user), None)
                if not name:
                    if isinstance(b, int) and b == -1:
                        return
                    if isinstance(b, int) and b == B:
                        pe.wait_ge(S["attn_out"], TILES * B - 1)
                    else:
                        wait(pe, S["lat_lo_done"], b + 1)
                    return
                t = at // 4
                semaphore, count = {
                    "attn": ("attn_out", 4 * b + t),
                    "max": ("mrest_done", 4 * b + t + 2),
                    "xT": ("xlo_done", 4 * (b + 1) + at - 1),
                    "qk": ("rest_done", 4 * (b + 1) + QK_SLOT.get(at, 0) + 1),
                    "v": ("logits_out", 4 * (b + 1) + at - V_SLOT + 1),
                    "latent": ("lat_lo_done", b + 2),
                    "gateT": ("cT_done", b + 1),
                }[name]
                wait(pe, S[semaphore], count)

            def split_matmul(to, xs, ws, done, column=None):
                n = 0
                for c in range(CH):
                    for i, j in ((0, 0), (0, 1), (1, 0)):
                        last = pe.matmul(to, xs(c)[i], ws(c)[j], start=(n == 0), stop=(column is None and n == 3 * CH - 1))
                        n += 1
                if column is not None:
                    last = pe.matmul(to, ones, bias[:, column:column + to.shape[-1]], start=False, stop=True)
                last.then_inc(S[done], 1)

            def weights(start, width):
                return lambda c: (w_hi[:, c, start:start + width], w_lo[:, c, start:start + width])

            def x_tile(par, t):
                return lambda c: (xT_hi[:, par, c, P * t:P * t + P], xT_lo[:, par, c, P * t:P * t + P])

            def x_row(par):
                return lambda c: (xT_hi[:, par, c, :], xT_lo[:, par, c, :])

            def scores_t(b, g, kt, s, i):
                n = 64 * b + 4 * s + i
                wait(pe, S["exp_done"], n - 1)
                h = GROUP * g + i
                pe.matmul(p2[i % 2][:, :], k_stack[:, h, P * kt:P * kt + P], q_stack[:, h, :],
                          start=True, stop=True).then_inc(S["st_done"], 1)

            def max_scores(u, g, i, qt):
                wait(pe, S["max_done"], 4 * u + qt - 1)
                h = GROUP * g + i
                pe.matmul(p1[qt % 2][:, :], q_stack[0:PRODUCTS * DH, h, P * qt:P * qt + P], k_stack[0:PRODUCTS * DH, h, :],
                          start=True, stop=True).then_inc(S["max_scores_done"], 1)

            def front(b, s, par, name):
                b1, par1 = b + 1, 1 - par
                if name == "attn":
                    wait(pe, S["av_out"], 4 * b + s // 4)
                    for qt in range(TILES):
                        last = pe.transpose(p_front[:, P * qt:P * qt + P], av[:, P * qt:P * qt + P], ident[:])
                    last.then_inc(S["attnT_done"], 1)
                if name == "max":
                    g = (s // 4 + 1) % 4
                    wait(pe, S["max_done"], 16 * (4 * b + s // 4 + 2))
                    pe.transpose(p_front[0:16, 0:P], negmax[:, g % 2, :], ident[:]).then_inc(S["maxT_done"], 1)
                if name == "xT":
                    t = s - 2
                    wait(pe, S["xn_done"], 4 * b1 + t + 1)
                    for c in range(CH):
                        last = pe.transpose(p_front[:, P * c:P * c + P], x_in[:, t, P * c:P * c + P], ident[:])
                    last.then_inc(S["xT_done"], 1)
                if name == "qk":
                    i = QK_SLOT[s]
                    start = QK + (i % 2) * D + (i // 2) * P
                    if i == 0:
                        wait(pe, S["xlo_done"], 4 * b1 + 4)
                        wait(pe, S["xhi_done"], 4 * b1 + 4)
                    split_matmul(p_front[:, :], weights(start, P), x_row(par1), "qk_done")
                if name == "v":
                    split_matmul(p_front[:, 0:D + E], x_tile(par1, s - V_SLOT), weights(VG, D + E), "v_done", BVG)
                if name == "latent":
                    split_matmul(p_front[:, :], weights(DD, 2 * L), x_row(par1), "latent_done")
                if name == "gateT":
                    wait(pe, S["cparts_done"], 2 * (b + 1))
                    for t in range(TILES):
                        last = pe.transpose(p_front[0:4 * E, P * t:P * t + P],
                                            c_parts[:, t, :, :].rearrange("p r e -> p (r e)"), ident[:])
                    last.then_inc(S["gateT_done"], 1)

            def mla_early(b, t, j, prev, body):
                tile = 4 * b + t
                if j == 1:
                    wait(pe, S["mkv_out"], tile + 1 if body else TILES * B)
                    if not body:
                        wait(pe, S["s_out"], tile - 2)
                    if prev if t == 0 else body:
                        if isinstance(b, int) or t != 0:
                            wait(pe, S["cT_done"], b + 1 if t else b)
                        bt = (t - 1) % 4
                        pe.matmul(p_mla[:, D:2 * D], cT[:, P * bt:P * bt + P], eb, start=True, stop=True).then_inc(S["bias_done"], 1)
                    if prev if t <= 1 else body:
                        wait(pe, S["mo_out"], tile - 1)
                        for c in range(CH):
                            last = pe.transpose(p_mla[:, P * c:P * c + P], mo[:, P * c:P * c + P], ident[:])
                        last.then_inc(S["moT_done"], 1)
                if j == 2:
                    wait(pe, S["z_half"], tile if body else TILES * B)
                    wait(pe, S["molo_done"], tile - 1)
                    wait(pe, S["mohi_done"], tile - 1)
                    split_matmul(p_mla[:, 0:D], lambda c: (moT_hi[:, c, :], moT_lo[:, c, :]), weights(WO, D), "wo_done", BOUT)

            def values(b, s, par):
                t, j = ((s - 1) // 4) % 4, (s - 1) % 4
                wait(pe, S["exp_done"], 4 * (16 * b + s))
                if s == 1:
                    wait(pe, S["v_out"], 4 * b + 4)
                if j == 0:
                    wait(pe, S["av_out"], 4 * b + t)
                for i in range(GROUP):
                    last = pe.matmul(p_av[32 * i:32 * i + DH + 1, :], v_one[:, par, j, GROUP * t + i, :],
                                     probs[:, (s - 1) % 2, i, :], start=(j == 0), stop=(j == 3))
                last.then_inc(S["av_done"], 1)

            def slot(b, s, par, prev, body, nxt):
                t, j = s // 4, s % 4
                n = 16 * b + s
                tile = 4 * b + t
                there, u, mg, mi = max_unit(b, s, body, nxt)
                early, late = front_bank_users(s, prev, body, nxt)
                if isinstance(b, int) and b == -1 and s in (6, 8, 15):
                    pe.wait_ge(S["wlo_done"], {6: 1, 8: 3, 15: 5}[s])
                    if s == 8:
                        pe.wait_ge(S["ones_out"], 1)
                        pe.wait_ge(S["bias_ready"], 16)
                if body:
                    if j == 0:
                        wait(pe, mrows[t % 2], 48 * (2 * b + t // 2 + 1))
                    if s == 0 and isinstance(b, int) and b == 0:
                        pe.wait_ge(S["wlo_done"], len(SPLIT_ORDER))
                        pe.wait_ge(S["eb_ready"], 16)
                    scores_t(b, t, j, s, 0)
                    scores_t(b, t, j, s, 1)
                if there and mi == 0 and mg in (0, 2):
                    wait(pe, stacked[mg // 2], STACKED * (b + 1 + (1 if mg == 0 else 0)))
                if there:
                    max_scores(u, mg, mi, 0)
                    max_scores(u, mg, mi, 1)
                if early:
                    front_bank_free(b, s, False, prev, body, nxt)
                    front(b, s, par, early)
                if (j == 1 and ((prev if t == 0 else body) or (prev and t == 1))) or (j == 2 and (prev if t <= 1 else body)):
                    mla_early(b, t, j, prev, body)
                if s not in LATE_VALUES and (prev if s == 0 else body):
                    values(b, s, 1 - par if s == 0 else par)
                if body:
                    scores_t(b, t, j, s, 2)
                    scores_t(b, t, j, s, 3)
                if j == 0 and body:
                    wait(pe, S["mq_out"], tile + 1)
                    if s == 0:
                        wait(pe, S["lat_lo_done"], b + 1)
                    pe.matmul(p_mla[:, :], latent[:, P * t:P * t + P], up_hi[:], start=True, stop=False)
                    pe.matmul(p_mla[:, :], latent[:, P * t:P * t + P], up_lo[:], start=False, stop=False)
                    pe.matmul(p_mla[:, :], ones, bias[:, BUP:BUP + 2 * D], start=False, stop=True).then_inc(S["mkv_done"], 1)
                if there:
                    max_scores(u, mg, mi, 2)
                    max_scores(u, mg, mi, 3)
                if body:
                    wait(pe, S["scaled_done"], 2 * n)
                    split_matmul(p_moe[:].rearrange("p e f -> p (e f)"), x_tile(par, t), weights(EX + 512 * j, 512), "moe_done")
                if s in LATE_VALUES and body:
                    values(b, s, par)
                if late:
                    front_bank_free(b, s, True, prev, body, nxt)
                    front(b, s, par, late)
                if j == 3 and (nxt if t == 3 else body):
                    wait(pe, S["s_out"], tile - 1)
                    wait(pe, S["mkv_out"], tile + 1)
                    wait(pe, S["z_half"], tile)
                    split_matmul(p_mla[:, 0:D], x_tile(1 - par, 0) if t == 3 else x_tile(par, t + 1), weights(MQ, D), "mq_done", BQ)

            pe.wait_ge(S["consts_done"], 1)
            pe.wait_ge(S["ones_done"], 1)
            pe.wait_ge(S["av_zeroed"], 1)
            pe.wait_ge(S["vones_done"], 2)
            batches(pe, slot)

        @block.scalar
        def _(act):
            def split(n):
                loads = {1: 2, 2: 2, 4: 2, 5: 2, 6: 2, 7: 2, UP: 2, EB: 4, BIAS: 5}
                act.wait_ge(w_loaded[n], 16 * loads.get(n, 1))
                for to, src in split_views(n, w_hi, up_hi[:], eb, bias):
                    last = act.activation(to, src, ACT.Copy)
                last.then_inc(S["whi_done"], 1)

            def exponentials(b, s, par, i):
                n = 64 * b + 4 * s + i
                wait(act, S["st_done"], n + 1)
                if i == 0:
                    wait(act, S["av_done"], 16 * b + s - 1)
                act.activation(probs[:, s % 2, i, :], p2[i % 2][:, :], ACT.Exp, scale=SCALE).then_inc(S["exp_done"], 1)

            def front(b, s, par, name):
                b1, par1 = b + 1, 1 - par
                if name == "max":
                    g = (s // 4 + 1) % 4
                    n = 4 * b + s // 4 + 1
                    wait(act, S["maxT_done"], n + 1)
                    wait(act, mrows[g % 2], 48 * (2 * b + (s // 4 + 1) // 2))
                    act.activation(mparts[:, g % 2, 0, :], p_front[0:16, 0:P], ACT.Copy).then_inc(S["m1_done"], 1)
                if name == "xT":
                    t = s - 2
                    wait(act, S["xT_done"], 4 * b1 + t + 1)
                    if t == 0:
                        wait(act, S["moe_done"], 16 * b)
                        wait(act, S["mq_done"], 4 * b)
                    act.activation(xT_hi[:, par1, :, P * t:P * t + P], p_front[:, 0:D].rearrange("p (c n) -> p c n", c=CH),
                                   ACT.Copy).then_inc(S["xhi_done"], 1)
                if name == "qk":
                    i = QK_SLOT[s]
                    n = 4 * b1 + i
                    wait(act, S["qk_done"], n + 1)
                    if i >= 2:
                        wait(act, stacked[0], STACKED * (b1 + 1))
                    else:
                        wait(act, stacked[1], STACKED * b1)
                    if isinstance(b, int) and b == -1 and i == 0:
                        act.wait_ge(S["bias_loaded"], 16 * 6)
                    act.activation(parts[:, i % 2, 0, :], p_front[:, :], ACT.Identity, bias=bqk[:, i:i + 1]).then_inc(S["part1_done"], 1)
                if name == "v":
                    t = s - V_SLOT
                    wait(act, S["v_done"], 4 * b1 + t + 1)
                    if t == 0:
                        wait(act, S["av_done"], 16 * b)
                    act.activation(v_one[:, par1, t, :, 0:DH], p_front[:, 0:D].rearrange("p (h d) -> p h d", h=H),
                                   ACT.Copy).then_inc(S["v_out"], 1)
                    if t == 0:
                        wait(act, S["gshift_done"], b1)
                    act.activation(logits[:, t, :], p_front[:, D:D + E], ACT.Copy).then_inc(S["logits_out"], 1)
                if name == "latent":
                    wait(act, S["latent_done"], b1 + 1)
                    wait(act, S["mkv_done"], 4 * b1)
                    act.activation(latent[:], p_front[:, :], ACT.Identity, bias=bdd[:, 0:1]).then_inc(S["lat_hi_done"], 1)
                if name == "gateT":
                    wait(act, S["gateT_done"], b + 1)
                    wait(act, S["bias_done"], 4 * b)
                    act.activation(cT, p_front[0:4 * E, :], ACT.Copy).then_inc(S["cT_done"], 1)

            def slot(b, s, par, prev, body, nxt):
                t, j = s // 4, s % 4
                n = 16 * b + s
                tile = 4 * b + t
                early, late = front_bank_users(s, prev, body, nxt)
                if body:
                    exponentials(b, s, par, 0)
                    exponentials(b, s, par, 1)
                if nxt and s - 1 in QK_SLOT:
                    i = QK_SLOT[s - 1]
                    wait(act, S["rest_done"], 4 * (b + 1) + i + 1)
                    act.activation(parts[:, i % 2, 1, :], rest[:], ACT.Copy).then_inc(S["part2_done"], 1)
                if j == 1 and (prev if t <= 1 else body):
                    wait(act, S["moT_done"], tile - 1)
                    wait(act, S["wo_done"], tile - 2)
                    act.activation(moT_hi[:], p_mla[:, 0:D].rearrange("p (c n) -> p c n", c=CH), ACT.Copy).then_inc(S["mohi_done"], 1)
                if j == 2 and (prev if t <= 1 else body):
                    wait(act, S["wo_done"], tile - 1)
                    if t >= 2:
                        wait(act, S["w_done"], tile - 5)
                    else:
                        wait(act, S["z_merged"], 4 * b - 1)
                    act.activation(s_mla[:, (t - 2) % 4, :], p_mla[:, 0:D], ACT.Copy).then_inc(S["s_out"], 1)
                if j == 0 and (prev if t == 0 else body):
                    wait(act, S["av_done"], n)
                    wait(act, S["attnT_done"], 4 * b + t - 1)
                    act.activation(av[:], p_av[:, :], ACT.Copy).then_inc(S["av_out"], 1)
                if early:
                    front(b, s, par, early)
                if body:
                    exponentials(b, s, par, 2)
                    exponentials(b, s, par, 3)
                if j == 0 and body:
                    wait(act, S["mkv_done"], tile + 1)
                    wait(act, S["value_products"], 2 * tile - 2)
                    act.activation(mkv[:, t % 2].rearrange("p r n -> p (r n)"), p_mla[:, :], ACT.Copy).then_inc(S["mkv_out"], 1)
                if prev and s in end_slots(body):
                    f = end_slots(body).index(s)
                    wait(act, S["z_ready"], b)
                    if f >= 2:
                        wait(act, S["res_done"], 4 * (b - 1) + f - 1)
                    act.activation(th[:, f % 2, :], z[:, f, :], ACT.Tanh, scale=0.5).then_inc(S["tanh_done"], 1)
                if nxt and 1 <= s <= 4:
                    k = s - 1
                    if k == 0:
                        wait(act, S["shift_done"], b + 2)
                    act.activation(x_in[:, k, :], x_in[:, k, :], ACT.Identity, bias=shift[:, 1, k:k + 1],
                                   scale=rstd[:, k:k + 1]).then_inc(S["xn_done"], 1)
                if body:
                    wait(act, S["moe_done"], n + 1)
                    for k in range(2):
                        e = 2 * j + k
                        if k == 0 and j == 0:
                            wait(act, S["z_merged"], tile - 1)
                        elif k == 0:
                            wait(act, S["moe_added"], 3 * tile + max(j - 2, 0))
                        act.activation(acc[:, t % 2, k, :] if j == 0 else scaled[:, j % 2, k, :], p_moe[:, k, :], ACT.Copy,
                                       scale=combine[:, par, t, e:e + 1]).then_inc(S["scaled_done"], 1)
                if late:
                    front(b, s, par, late)
                if j == 3 and body:
                    wait(act, S["mshift_done"], tile + 1)
                    act.activation(msc[:, t % 2], msc[:, t % 2], ACT.Exp, scale=SCALE).then_inc(S["mexp_done"], 1)
                if s == 12 and nxt:
                    wait(act, S["gshift_done"], b + 2)
                    act.activation(gate[:], gshift[:], ACT.Exp).then_inc(S["gexp_done"], 1)
                if j == 3 and (nxt if t == 3 else body):
                    wait(act, S["mq_done"], tile + 2)
                    wait(act, S["score_products"], 2 * tile + 2)
                    act.activation(mq[:], p_mla[:, 0:D], ACT.Copy).then_inc(S["mq_out"], 1)
                if isinstance(b, int) and b == -1:
                    for k in SPLITS.get(s, ()):
                        split(k)

            batches(act, slot)

        @block.vector
        def _(dve):
            def split(n):
                dve.wait_ge(S["whi_done"], SPLIT_ORDER.index(n) + 1)
                for (to, src), (high, _) in zip(split_views(n, w_lo, up_lo[:], eb_low, bias_low),
                                                split_views(n, w_hi, up_hi[:], eb, bias)):
                    last = dve.tensor_tensor(to, src, high.bitcast(F32), ALU.subtract)
                last.then_inc(S["wlo_done"], 1)

            attn_heads = p_front[:, :].rearrange("p (q h r) -> p q h r", q=TILES, h=GROUP)

            def row_max(u, mg, mi, qt):
                wait(dve, S["max_scores_done"], 4 * u + qt + 1)
                if mi == 0 and qt == 0:
                    wait(dve, S["maxT_done"], front_group(u) - 1)
                dve.tensor_reduce(negmax[:, mg % 2, 4 * mi + qt:4 * mi + qt + 1], p1[qt % 2][:, :], AX, ALU.max,
                                  negate=True).then_inc(S["max_done"], 1)

            def front_group(u):
                return u // 4 if isinstance(u, int) else u_group[0]

            u_group = [0]

            def sum_scores(tile, m, lo):
                wait(dve, S["score_products"], 2 * tile + lo + 1)
                if lo == 0:
                    wait(dve, S["value_products"], 2 * tile - 2)
                dve.tensor_reduce(msc[:, m, 8 * lo:8 * lo + 8, :].rearrange("p h g -> p (h g)"),
                                  prod[:, 1 - lo, :].rearrange("p (a d) -> p a d", d=DH), AX, ALU.add).then_inc(S["scores_reduced"], 1)

            def sum_values(tile, lo):
                wait(dve, S["value_products"], 2 * tile + lo + 1)
                if lo == 0:
                    wait(dve, S["moT_done"], tile)
                dve.tensor_reduce(mo[:, P * lo:P * lo + P], prod[:, lo, :].rearrange("p (a g) -> p a g", g=H),
                                  AX, ALU.add).then_inc(S["values_reduced"], 1)

            def attn_reciprocal(b, s):
                n = 4 * b + s // 4
                wait(dve, S["attnT_done"], n)
                wait(dve, S["attn_out"], n - 1)
                dve.reciprocal(arec[:], attn_heads[:, :, :, DH]).then_inc(S["arec_done"], 1)

            def attn_normalise(b, s):
                n = 4 * b + s // 4
                g = (s // 4 - 1) % 4
                wait(dve, S["arec_done"], n)
                if s == 5:
                    wait(dve, S["z_ready"], b)
                dve.tensor_tensor(attn[:, :, GROUP * DH * g:GROUP * DH * (g + 1)].rearrange("p q (h d) -> p q h d", h=GROUP),
                                  attn_heads[:, :, :, 0:DH], arec[:].unsqueeze(3).broadcast_to([P, TILES, GROUP, DH]),
                                  ALU.mult).then_inc(S["attn_out"], 1)

            def max_rest(b, s):
                g, n = (s // 4 + 1) % 4, 4 * b + s // 4 + 1
                wait(dve, S["m1_done"], n + 1)
                wait(dve, S["m3_done"], n)
                dve.tensor_tensor(mrest[:], p_front[0:16, 0:P], mparts[:, g % 2, 0, :], ALU.subtract).then_inc(S["mrest_done"], 1)

            def max_second(b, s):
                g, n = (s // 4 + 1) % 4, 4 * b + s // 4 + 1
                wait(dve, S["mrest_done"], n + 1)
                dve.tensor_copy(mparts[:, g % 2, 1, :], mrest[:]).then_inc(S["m2_done"], 1)

            def max_third(b, s):
                g, n = (s // 4 + 1) % 4, 4 * b + s // 4 + 1
                wait(dve, S["m2_done"], n + 1)
                dve.tensor_tensor(mparts[:, g % 2, 2, :], mrest[:], mparts[:, g % 2, 1, :], ALU.subtract).then_inc(S["m3_done"], 1)

            def x_low(b, s, par):
                b1, t = b + 1, s - 2
                wait(dve, S["xhi_done"], 4 * b1 + t + 1)
                at = (slice(None), 1 - par, slice(None), slice(P * t, P * t + P))
                dve.tensor_tensor(xT_lo[at], p_front[:, 0:D].rearrange("p (c n) -> p c n", c=CH), xT_hi[at].bitcast(F32),
                                  ALU.subtract).then_inc(S["xlo_done"], 1)

            def qk_rest(b, s):
                b1, i = b + 1, QK_SLOT[s]
                n = 4 * b1 + i
                wait(dve, S["part1_done"], n + 1)
                wait(dve, S["part3_done"], n)
                if isinstance(b, int) and b == -1 and i == 0:
                    dve.wait_ge(S["bias_loaded"], 16 * 6)
                dve.scalar_tensor_tensor(out=rest[:], in0=p_front[:, :], scalar=bqk[:, i:i + 1], in1=parts[:, i % 2, 0, :],
                                         op0=ALU.add, op1=ALU.subtract).then_inc(S["rest_done"], 1)

            def latent_low(b, s):
                wait(dve, S["lat_hi_done"], b + 2)
                dve.scalar_tensor_tensor(out=latent[L:P, :], in0=p_front[L:P, :], scalar=bdd[L:P, 0:1],
                                         in1=latent[L:P, :].bitcast(F32), op0=ALU.add, op1=ALU.subtract).then_inc(S["lat_lo_done"], 1)

            def gate_softmax(b1):
                wait(dve, S["logits_out"], 4 * b1 + 4)
                dve.tensor_reduce(gsum[:], logits[:], AX, ALU.max).then_inc(S["gmax_done"], 1)
                wait(dve, S["gmax_done"], b1 + 1)
                wait(dve, S["combine_done"], b1)
                dve.tensor_tensor(gshift[:], logits[:], gsum[:].unsqueeze(2).broadcast_to([P, TILES, E]), ALU.subtract).then_inc(S["gshift_done"], 1)

            def gate_sum(b1):
                wait(dve, S["gexp_done"], b1 + 1)
                dve.tensor_reduce(gsum[:], gate[:], AX, ALU.add).then_inc(S["gsum_done"], 1)

            def gate_reciprocal(b1):
                wait(dve, S["gsum_done"], b1 + 1)
                dve.reciprocal(gsum[:], gsum[:]).then_inc(S["grec_done"], 1)

            def gate_normalise(b1):
                wait(dve, S["grec_done"], b1 + 1)
                dve.tensor_tensor(gate[:], gate[:], gsum[:].unsqueeze(2).broadcast_to([P, TILES, E]), ALU.mult).then_inc(S["gate_done"], 1)

            def gate_top(b1):
                wait_apart(dve, S["dve_passed"], S["gate_done"], b1 + 1)
                for t in range(TILES):
                    dve.max(top[:, t, :], gate[:, t, :]).then_inc(S["top_done"], 1)

            def gate_index(b1):
                wait_apart(dve, S["dve_passed"], S["top_done"], 4 * b1 + 4)
                for t in range(TILES):
                    dve.max_index(topi[:, t, :], top[:, t, :], gate[:, t, :]).then_inc(S["topi_done"], 1)

            def gate_index_float(b1):
                wait(dve, S["topi_done"], 4 * b1 + 4)
                dve.tensor_copy(topf[:], topi[:, :, 0:2]).then_inc(S["topf_done"], 1)

            def gate_pick(b1):
                wait(dve, S["topf_done"], b1 + 1)
                for k in range(2):
                    dve.tensor_tensor(pick[:, k, :, :], iota[:], topf[:, :, k:k + 1].broadcast_to([P, TILES, E]), ALU.is_equal).then_inc(S["pick_done"], 1)

            def gate_both(b1):
                wait(dve, S["pick_done"], 2 * (b1 + 1))
                dve.tensor_tensor(pick[:, 0, :, :], pick[:, 0, :, :], pick[:, 1, :, :], ALU.add).then_inc(S["picks_done"], 1)

            def gate_combine(b, b1, par1):
                wait(dve, S["picks_done"], b1 + 1)
                wait(dve, S["scaled_done"], 32 * b)
                dve.tensor_tensor(combine[:, par1, :, :], gate[:], pick[:, 0, :, :], ALU.mult).then_inc(S["combine_done"], 1)

            def gate_high(b1, par1):
                wait(dve, S["combine_done"], b1 + 1)
                wait(dve, S["gateT_done"], b1)
                dve.tensor_copy(c_hi[:], combine[:, par1, :, :]).then_inc(S["chi_done"], 1)

            def gate_parts(b1, par1):
                wait(dve, S["chi_done"], b1 + 1)
                both = [P, TILES, 2, E]
                dve.tensor_copy(c_parts[:, :, 0::2, :], c_hi[:].bitcast(F32).unsqueeze(2).broadcast_to(both)).then_inc(S["cparts_done"], 1)
                dve.tensor_tensor(c_parts[:, :, 1::2, :], combine[:, par1, :, :].unsqueeze(2).broadcast_to(both),
                                  c_hi[:].bitcast(F32).unsqueeze(2).broadcast_to(both), ALU.subtract).then_inc(S["cparts_done"], 1)

            def slot(b, s, par, prev, body, nxt):
                t, j = s // 4, s % 4
                tile = 4 * b + t
                two_before = prev if t <= 1 else body
                b1, par1 = b + 1, 1 - par
                there, u, mg, mi = max_unit(b, s, body, nxt)
                u_group[0] = 4 * b + (s + 6) // 4
                early, late = front_bank_users(s, prev, body, nxt)
                if there:
                    row_max(u, mg, mi, 0)
                    row_max(u, mg, mi, 1)
                if s == 14 and nxt:
                    gate_reciprocal(b1)
                if s == 15 and nxt:
                    gate_index(b1)
                if isinstance(b, int) and b == -1:
                    for k in SPLITS.get(s - 1, ()):
                        split(k)
                if early == "attn":
                    attn_reciprocal(b, s)
                if j == 0 and (prev if t == 0 else body):
                    wait(dve, S["mexp_done"], tile)
                    dve.tensor_reduce(msum[:], msc[:, (t - 1) % 2], AX, ALU.add).then_inc(S["msum_done"], 1)
                if j == 0 and two_before:
                    sum_values(tile - 2, 1)
                if j == 0 and (prev if t == 0 else body):
                    wait(dve, S["msum_done"], tile)
                    wait(dve, S["mo_out"], tile - 2)
                    dve.reciprocal(mrec[:, (t - 1) % 2, :], msum[:]).then_inc(S["mrec_done"], 1)
                if j == 1 and two_before:
                    wait(dve, S["mohi_done"], tile - 1)
                    wait(dve, S["wo_done"], tile - 2)
                    dve.tensor_tensor(moT_lo[:], p_mla[:, 0:D].rearrange("p (c n) -> p c n", c=CH), moT_hi[:].bitcast(F32),
                                      ALU.subtract).then_inc(S["molo_done"], 1)
                if early == "attn":
                    attn_normalise(b, s)
                if j == 1 and (prev if t == 0 else body):
                    wait(dve, S["moe_added"], 3 * tile)
                    wait(dve, S["bias_done"], tile)
                    if t == 0:
                        wait(dve, S["z_merged"], 4 * b - 1)
                    else:
                        wait(dve, S["g_done"], tile - 4)
                    zt = z[:, (t - 1) % 4, :]
                    dve.tensor_tensor(zt, acc[:, (t - 1) % 2, 0, :], p_mla[:, D:2 * D], ALU.add).then_inc(S["z_half"], 1)
                    sum_values(tile - 1, 0)
                if j == 2 and body:
                    sum_scores(tile, t % 2, 0)
                if j == 3 and body:
                    sum_scores(tile, t % 2, 1)
                if early == "latent":
                    latent_low(b, s)
                if early == "max":
                    max_rest(b, s)
                if s == 15 and nxt:
                    gate_index_float(b1)
                if there:
                    row_max(u, mg, mi, 2)
                if early == "max":
                    max_second(b, s)
                if j == 3 and body:
                    wait(dve, S["scores_reduced"], 2 * tile + 2)
                    dve.tensor_reduce(mmax[:], msc[:, t % 2], AX, ALU.max).then_inc(S["mmax_done"], 1)
                if j == 0 and two_before:
                    wait(dve, S["values_reduced"], 2 * tile - 2)
                    wait(dve, S["mrec_done"], tile - 1)
                    dve.tensor_tensor(mo[:].rearrange("p (h d) -> p h d", h=H), mo[:].rearrange("p (h d) -> p h d", h=H),
                                      mrec[:, t % 2, :].unsqueeze(2).broadcast_to([P, H, DH]), ALU.mult).then_inc(S["mo_out"], 1)
                if s == 14 and nxt:
                    gate_normalise(b1)
                if s == 15 and nxt:
                    gate_pick(b1)
                if there:
                    row_max(u, mg, mi, 3)
                if s == 15 and nxt:
                    gate_both(b1)
                if j == 3 and body:
                    wait(dve, S["mmax_done"], tile + 1)
                    dve.tensor_tensor(msc[:, t % 2], msc[:, t % 2], mmax[:].unsqueeze(2).broadcast_to([P, H, H]), ALU.subtract).then_inc(S["mshift_done"], 1)
                if early == "max":
                    max_third(b, s)
                if s == 15 and nxt:
                    gate_combine(b, b1, par1)
                if late == "xT":
                    x_low(b, s, par)
                if late == "qk":
                    qk_rest(b, s)
                if j == 1 and (prev if t == 0 else body):
                    zt = z[:, (t - 1) % 4, :]
                    wait(dve, S["z_half"], tile)
                    dve.tensor_tensor(zt, zt, acc[:, (t - 1) % 2, 1, :], ALU.add).then_inc(S["z_merged"], 1)
                if s == 15 and nxt:
                    gate_high(b1, par1)
                if nxt and s == 0:
                    wait(dve, S["x_loaded"], 16 * (b1 + 1))
                    for k in range(TILES):
                        dve.bn_stats(stats[:, k, :], x_in[:, k, :]).then_inc(S["stats_done"], 1)
                    wait(dve, S["stats_done"], 4 * (b1 + 1))
                    wait_apart(dve, S["dve_passed"], S["xn_done"], 4 * b1)
                    wait_apart(dve, S["dve_passed"], S["ve_done"], b1)
                    wait_apart(dve, S["dve_passed"], S["neg_done"], b1)
                    for k in range(TILES):
                        dve.bn_aggr(meanvar[:, k, :], stats[:, k, :]).then_inc(S["meanvar_done"], 1)
                if s == 12 and nxt:
                    gate_softmax(b1)
                if s == 13 and nxt:
                    gate_sum(b1)
                if s == 14 and nxt:
                    gate_top(b1)
                if s == 15 and nxt:
                    gate_parts(b1, par1)
                if prev and s in end_slots(body):
                    f = end_slots(body).index(s)
                    n = 4 * (b - 1) + f
                    wait(dve, S["tanh_done"], n + 1)
                    dve.scalar_tensor_tensor(out=th[:, f % 2, :], in0=th[:, f % 2, :], scalar=1.0, in1=z[:, f, :],
                                             op0=ALU.add, op1=ALU.mult).then_inc(S["g_done"], 1)
                    wait(dve, S["g_done"], n + 1)
                    wait(dve, S["s_out"], n + 1)
                    dve.scalar_tensor_tensor(out=th[:, f % 2, :], in0=th[:, f % 2, :], scalar=0.5, in1=s_mla[:, f, :],
                                             op0=ALU.mult, op1=ALU.mult).then_inc(S["w_done"], 1)

            dve.memset(p_av[:, :], 0.0).then_inc(S["av_zeroed"], 1)
            dve.wait_ge(S["consts_done"], 1)
            dve.tensor_scalar(ones, ident[4 * E:4 * E + 2, :], 0.0, 1.0, ALU.mult, ALU.add).then_inc(S["ones_out"], 1)
            dve.wait_ge(S["iota_done"], 1)
            batches(dve, slot)

        @block.gpsimd
        def _(pool):
            def score_product(tile, m, lo):
                heads = slice(8 * lo, 8 * lo + 8)
                shape = [P, 8, H, H]
                if lo == 0:
                    wait(pool, S["mkv_out"], tile + 1)
                wait(pool, S["values_reduced"], 2 * tile - 2 + lo)
                pool.tensor_tensor(prod[:, 1 - lo, :].rearrange("p (h g d) -> p h g d", h=8, g=H),
                                   mq[:].rearrange("p (h d) -> p h d", h=H)[:, heads, :].unsqueeze(2).broadcast_to(shape),
                                   mkv[:, m, 0, :].rearrange("p (g d) -> p g d", g=H).unsqueeze(1).broadcast_to(shape),
                                   ALU.mult).then_inc(S["score_products"], 1)

            def value_product(tile, m, lo, body):
                heads = slice(8 * lo, 8 * lo + 8)
                shape = [P, 8, H, H]
                if lo == 0:
                    wait(pool, S["mexp_done"], tile + 1)
                if lo == 0 or body:
                    wait(pool, S["scores_reduced"], 2 * tile + 2 + lo)
                else:
                    wait(pool, S["values_reduced"], 2 * tile)
                pool.tensor_tensor(prod[:, lo, :].rearrange("p (h d g) -> p h d g", h=8, d=H),
                                   msc[:, m, heads, :].unsqueeze(2).broadcast_to(shape),
                                   mkv[:, m, 1, :].rearrange("p (d g) -> p d g", d=DH).unsqueeze(1).broadcast_to(shape),
                                   ALU.mult).then_inc(S["value_products"], 1)

            def add_experts(n, tile, j, m):
                wait(pool, S["scaled_done"], 2 * n + 2)
                wait(pool, S["moe_added"], 3 * tile + j - 1)
                pool.tensor_tensor(acc[:, m], acc[:, m], scaled[:, j % 2], ALU.add).then_inc(S["moe_added"], 1)

            def slot(b, s, par, prev, body, nxt):
                t, j = s // 4, s % 4
                tile = 4 * b + t
                n = 16 * b + s
                before = prev if t == 0 else body
                b1 = b + 1
                if j == 0 and before:
                    value_product(tile - 1, (t - 1) % 2, 0, body)
                if j in (1, 2) and body:
                    score_product(tile, t % 2, j - 1)
                if (j == 3 if body else s == 1) and before:
                    value_product(tile - 1, (t - 1) % 2, 1, body)
                if nxt and s - 1 in QK_SLOT:
                    i = QK_SLOT[s - 1]
                    wait(pool, S["part2_done"], 4 * b1 + i + 1)
                    pool.tensor_tensor(parts[:, i % 2, 2, :], rest[:], parts[:, i % 2, 1, :], ALU.subtract).then_inc(S["part3_done"], 1)
                if j != 1 and (prev if s == 0 else body):
                    add_experts(n - 1, tile - 1 if j == 0 else tile, (j - 1) % 4, (t - 1 if j == 0 else t) % 2)
                if nxt and s == 1:
                    wait(pool, S["meanvar_done"], 4 * (b1 + 1))
                    wait_apart(pool, S["pool_passed"], S["rstd_done"], b1)
                    pool.tensor_scalar(vareps[:], meanvar[:, :, 1], EPS, None, ALU.add).then_inc(S["ve_done"], 1)
                    wait(pool, S["ve_done"], b1 + 1)
                    wait(pool, S["xn_done"], 4 * b1)
                    pool.tensor_tensor(rstd[:], vareps[:], half[:], ALU.pow).then_inc(S["rstd_done"], 1)
                    wait_apart(pool, S["pool_passed"], S["shift_done"], b1)
                    pool.tensor_scalar(shift[:, 0, :], meanvar[:, :, 0], -1.0, None, ALU.mult).then_inc(S["neg_done"], 1)
                    wait(pool, S["rstd_done"], b1 + 1)
                    wait(pool, S["neg_done"], b1 + 1)
                    pool.tensor_tensor(shift[:, 1, :], shift[:, 0, :], rstd[:], ALU.mult).then_inc(S["shift_done"], 1)
                if prev and s == 2:
                    wait(pool, S["attn_out"], 4 * b)
                    wait(pool, S["z_merged"], 4 * b)
                    pool.tensor_tensor(z[:], z[:], attn[:], ALU.add).then_inc(S["z_ready"], 1)
                if prev and s - 1 in end_slots(body):
                    f = end_slots(body).index(s - 1)
                    wait(pool, S["w_done"], 4 * (b - 1) + f + 1)
                    wait(pool, xfin_loaded[f % 2], 16 * (2 * (b - 1) + f // 2 + 1))
                    pool.tensor_tensor(x_fin[:, f % 2, :], th[:, f % 2, :], x_fin[:, f % 2, :], ALU.add).then_inc(S["res_done"], 1)

            pool.memset(ident[:], 0.0).then_inc(S["ident_zeroed"], 1)
            pool.wait_ge(S["ident_zeroed"], 1)
            pool.affine_select(out=ident[:], in_=ident[:], compare_op=ALU.not_equal, fill=1.0, base=0,
                               pattern=[[-1, P]], channel_multiplier=1).then_inc(S["consts_done"], 1)
            pool.memset(half[:], -0.5).then_inc(S["half_done"], 1)
            pool.iota(iota[:], pattern=[[0, TILES], [1, E]], base=0, channel_multiplier=0,
                      allow_small_or_imprecise_dtypes=True).then_inc(S["iota_done"], 1)
            for p in range(2):
                pool.memset(v_one[:, p, :, :, DH:DH + 1], 1.0).then_inc(S["vones_done"], 1)
            pool.wait_ge(S["vones_done"], 2)
            pool.memset(k_stack[PRODUCTS * DH:ROWS, :, :], 1.0).then_inc(S["ones_done"], 1)
            pool.wait_ge(S["ones_done"], 1)
            pool.wait_ge(S["half_done"], 1)
            batches(pool, slot)


_INS = ["L0_attn_x", "L0_attn_Wq", "L0_attn_bq", "L0_attn_Wdown", "L0_attn_bdown", "L0_attn_Wup", "L0_attn_bup", "L0_attn_Wout",
        "L0_attn_bout", "L0_ffn_W_qkv", "L0_ffn_b_qkv", "L0_ffn_W_gate", "L0_ffn_b_gate", "L0_ffn_W_experts", "L0_ffn_b_experts"]


def kernel(**inputs):
    import numpy as np
    import concourse.bacc as bacc
    from concourse import mybir as m
    from concourse.bass_utils import run_bass_kernel_spmd

    nc = bacc.Bacc("TRN2", target_bir_lowering=False, num_devices=1)
    arrays, args = {}, []
    for name in _INS:
        a = np.ascontiguousarray(inputs[name])
        arrays[f"in_{name}"] = a
        args.append(nc.dram_tensor(f"in_{name}", a.shape, m.dt.from_np(a.dtype), kind="ExternalInput").ap())
    out = nc.dram_tensor("out", inputs["L0_attn_x"].shape, m.dt.float32, kind="ExternalOutput").ap()
    build(nc, *args, out)
    return run_bass_kernel_spmd(nc, [arrays], core_ids=[0]).results[0]["out"]
```
